# Optimizing a Trainium2 kernel written in Bass

```python
import numpy as np
import jax
import jax.numpy as jnp

def _softmax(x, axis=-1):
    return jax.nn.softmax(x, axis=axis)

def _gelu(x):
    return jax.nn.gelu(x, approximate=True)

def _silu(x):
    return jax.nn.silu(x)

def _sigmoid(x):
    return jax.nn.sigmoid(x)

def _layernorm(x, axis=-1, eps=1e-05):
    m = jnp.mean(x, axis=axis, keepdims=True)
    v = jnp.var(x, axis=axis, keepdims=True)
    return (x - m) / jnp.sqrt(v + eps)

def _scatter_add(tgt, idx, src, axis=0):
    return tgt.at[idx].add(src)

def _segment_sum(src, seg, n):
    return jax.ops.segment_sum(src, seg, n)
kernel_name = 'mk_flamingo_gated_d1_seqx_r4_e39b7e'

def setup_inputs(seed: int=0):
    np.random.seed(seed)
    _w = jnp.asarray

    def _rec_inputs():
        import jax
        import jax.numpy as jnp
        _rk = jax.random.key(seed)
        x = -0.000929 + 1 * jax.random.normal(jax.random.fold_in(_rk, 1), (8, 512, 256), jnp.float32)
        _lenS = 512 - jax.random.randint(jax.random.fold_in(_rk, 7), (8,), 0, max(1, 512 // 4) + 1, jnp.int32)
        _lenS2 = 1601 - jax.random.randint(jax.random.fold_in(_rk, 8), (8,), 0, max(1, 1601 // 4) + 1, jnp.int32)
        _ctx_1024P = jax.random.normal(jax.random.fold_in(_rk, 11), (8, 16, 256), jnp.float32)
        _ctx_1024c = jax.random.dirichlet(jax.random.fold_in(_rk, 511), 0.3 * jnp.ones((16,), jnp.float32), (8, 1601))
        _ctx_1024t = jnp.einsum('bsk,bkd->bsd', _ctx_1024c, _ctx_1024P)
        _ctx_1024t = _ctx_1024t * jax.lax.rsqrt(jnp.mean(jnp.square(_ctx_1024t)) + 1e-12) * 0.953939
        ctx_1024 = -1.52775e-05 + 0.999936 * (_ctx_1024t + 0.3 * jax.random.normal(jax.random.fold_in(_rk, 611), (8, 1601, 256), jnp.float32))
        _g = jax.random.normal(jax.random.fold_in(_rk, 9001), (2, 1), jnp.float32)
        _g = jnp.sign(_g) * jnp.maximum(jnp.abs(_g), 1.0) + (_g == 0) * 1.0
        g_xattn = _g[0]
        g_ffn = _g[1]
        return (x, ctx_1024, g_xattn, g_ffn)
    x, ctx_1024, g_xattn, g_ffn = _rec_inputs()

    def _L0_xattn_setup():
        import jax, jax.numpy as jnp
        import numpy as np
        B, N, L, D, H = (8, 128, 1024, 256, 16)
        key = jax.random.key(seed)
        ks = jax.random.split(key, 7)
        s = 1.0 / np.sqrt(D)
        return {'q': jax.random.normal(ks[0], (B, N, D), dtype=jnp.float32), 'k': jax.random.normal(ks[1], (B, L, D), dtype=jnp.float32), 'v': jax.random.normal(ks[2], (B, L, D), dtype=jnp.float32), 'Wq': jax.random.normal(ks[3], (D, D), dtype=jnp.float32) * s, 'Wk': jax.random.normal(ks[4], (D, D), dtype=jnp.float32) * s, 'Wv': jax.random.normal(ks[5], (D, D), dtype=jnp.float32) * s, 'Wo': jax.random.normal(ks[6], (D, D), dtype=jnp.float32) * s}
    _L0_xattn_all = _L0_xattn_setup()
    _L0_xattn_in = {k: v for k, v in _L0_xattn_all.items() if k in ('Wq', 'Wk', 'Wv', 'Wo')}
    del _L0_xattn_all

    def _L0_ffn_setup():
        import jax, jax.numpy as jnp
        import numpy as np
        N_EXPERTS = 8
        TOP_K = 2
        key = jax.random.key(seed)
        k1, k2, k3, k4 = jax.random.split(key, 4)
        B, T, C, H, E = (2, 512, 256, 1024, N_EXPERTS)
        x = jax.random.normal(k1, (B, T, C), dtype=jnp.float32)
        router_w = jax.random.normal(k2, (E, C), dtype=jnp.float32) * 0.02
        w1 = jax.random.normal(k3, (E, C, H), dtype=jnp.float32) * (1.0 / np.sqrt(C))
        w2 = jax.random.normal(k4, (E, H, C), dtype=jnp.float32) * (1.0 / np.sqrt(H))
        return {'x': x, 'router_w': router_w, 'w1': w1, 'w2': w2}
    _L0_ffn_all = _L0_ffn_setup()
    _L0_ffn_in = {k: v for k, v in _L0_ffn_all.items() if k in ('router_w', 'w1', 'w2')}
    del _L0_ffn_all
    return {'x': x, 'ctx_1024': ctx_1024, 'g_xattn': g_xattn, 'g_ffn': g_ffn, 'L0_xattn_Wq': _L0_xattn_in['Wq'], 'L0_xattn_Wk': _L0_xattn_in['Wk'], 'L0_xattn_Wv': _L0_xattn_in['Wv'], 'L0_xattn_Wo': _L0_xattn_in['Wo'], 'L0_ffn_router_w': _L0_ffn_in['router_w'], 'L0_ffn_w1': _L0_ffn_in['w1'], 'L0_ffn_w2': _L0_ffn_in['w2']}

def reference(x, ctx_1024, g_xattn, g_ffn, L0_xattn_Wq, L0_xattn_Wk, L0_xattn_Wv, L0_xattn_Wo, L0_ffn_router_w, L0_ffn_w1, L0_ffn_w2):
    import jax
    import jax.numpy as jnp

    def _L0_xattn_ref(q, k, v, Wq, Wk, Wv, Wo):
        import jax, jax.numpy as jnp
        import numpy as np
        B, N, L, D, H = (8, 128, 1024, 256, 16)
        Bq, Nq, Dm = q.shape
        Lk = k.shape[1]
        Hh = H
        Dh = Dm // Hh
        scale = Dm ** (-0.5)
        qh = (q @ Wq.T).reshape(Bq, Nq, Hh, Dh).transpose(0, 2, 1, 3)
        kh = (k @ Wk.T).reshape(Bq, Lk, Hh, Dh).transpose(0, 2, 1, 3)
        vh = (v @ Wv.T).reshape(Bq, Lk, Hh, Dh).transpose(0, 2, 1, 3)
        attn = jnp.einsum('bhnc,bhlc->bhnl', qh * scale, kh)
        attn = jax.nn.softmax(attn, axis=2)
        attn = attn / jnp.sum(attn, axis=-1, keepdims=True)
        out = jnp.einsum('bhnl,bhlc->bhnc', attn, vh)
        out = out.transpose(0, 2, 1, 3).reshape(Bq, Nq, Dm)
        return out @ Wo.T

    def _L0_ffn_ref(x, router_w, w1, w2):
        import jax, jax.numpy as jnp
        import numpy as np
        N_EXPERTS = 8
        TOP_K = 2
        B, T, C = x.shape
        E = N_EXPERTS
        xf = x.reshape(-1, C)
        logits = jnp.einsum('nc,ec->ne', xf, router_w)
        probs = jax.nn.softmax(logits, axis=-1)
        top_w, top_i = jax.lax.top_k(probs, TOP_K)
        top_w = top_w / jnp.sum(top_w, axis=-1, keepdims=True)
        comb = jnp.einsum('nk,nke->ne', top_w, jax.nn.one_hot(top_i, E, dtype=xf.dtype))
        h = jax.nn.gelu(jnp.einsum('nc,ech->enh', xf, w1), approximate=False)
        y = jnp.einsum('enh,ehc->enc', h, w2)
        out = jnp.einsum('ne,enc->nc', comb, y)
        return out.reshape(B, T, C)
    x = x + jnp.tanh(g_xattn[0]) * _L0_xattn_ref(_layernorm(x, axis=-1), ctx_1024, ctx_1024, L0_xattn_Wq, L0_xattn_Wk, L0_xattn_Wv, L0_xattn_Wo)
    x = x + jnp.tanh(g_ffn[0]) * _L0_ffn_ref(_layernorm(x, axis=-1), L0_ffn_router_w, L0_ffn_w1, L0_ffn_w2)
    return x

_drawn_inputs = setup_inputs


def setup_inputs(seed=0):
    import zlib

    import numpy as np

    out = dict(_drawn_inputs(seed))
    spreads = {}
    factors = {}
    for name, (base, spread) in spreads.items():
        noise = np.random.default_rng([zlib.crc32(name.encode()), seed]).standard_normal(out[name].shape)
        drawn = base * np.exp(spread * noise) if base else spread * noise
        out[name] = jnp.asarray(drawn.astype(out[name].dtype))
    for name, factor in factors.items():
        out[name] = (out[name] * factor).astype(out[name].dtype)
    return out
```

```python
from contextlib import ExitStack

import concourse.bass as bass
from concourse import mybir

ALU = mybir.AluOpType
ACT = mybir.ActivationFunctionType
AX = mybir.AxisListType
F32 = mybir.dt.float32
BF16 = mybir.dt.bfloat16
I32 = mybir.dt.int32
U32 = mybir.dt.uint32
SP_ENGINE = mybir.EngineType.SP

P = 128
B, N, D = 8, 512, 256
L = 1601
H = 16
DH = D // H
E, HID = 8, 1024
EPS = 1e-5
KC = D // P
NT = N // P
LT = (L + P - 1) // P
GH = 4
G = H // GH
STEPS = G * LT
UNITS = 2 * STEPS
RING = 4
SLOTS = 3
K_PART = (0, 0, 0, 1, 1, 1, 2, 2)
Q_PART = (0, 1, 2, 0, 1, 2, 0, 1)
BLOCKS = len(K_PART)
KCHUNK = 4
KCOLS = [(L * i) // KCHUNK for i in range(KCHUNK + 1)]
KCMAX = max(KCOLS[i + 1] - KCOLS[i] for i in range(KCHUNK))
CHUNKS = KC + KC * KCHUNK
VF = (LT + 1) // 2
TOKENS = B * N
ROW = D + 2
BLK = 256
REGION = TOKENS + BLK
SPARE = E * REGION
NBLK = (2 * TOKENS) // BLK + E - 1
LOADS = 16 * 2 * BLOCKS

FILL_AT = {
    3: ("tail", "o_turn", 3), 4: ("tail", "attn_turn", 0), 5: ("tail", "attn_turn", 1),
    6: ("tail", "out_proj", 0), 7: ("tail", "out_proj", 1),
    9: ("next", "x_turn", 0), 10: ("next", "x_turn", 1),
    11: ("tail", "row_turn", 0), 12: ("tail", "row_turn", 1), 13: ("tail", "logits", 0),
    14: ("next", "q", 0), 15: ("next", "q", 1),
    16: ("cur", "o_turn", 0),
    17: ("next", "k", 0), 18: ("next", "k", 1), 19: ("tail", "prefix", 0),
    20: ("next", "k", 2), 22: ("next", "k", 3), 24: ("next", "k", 4), 26: ("next", "k", 5),
    28: ("next", "k", 6), 29: ("cur", "o_turn", 1), 31: ("next", "k", 7),
    33: ("next", "v", 0), 35: ("next", "v", 1), 37: ("next", "v", 2), 39: ("next", "v", 3),
    41: ("next", "v", 4), 42: ("cur", "o_turn", 2), 44: ("next", "v", 5), 46: ("next", "v", 6),
}


class Iteration:

    def __init__(self, b, tail=True, cur=True, nxt=True):
        self.b, self.tail, self.cur, self.next = b, tail, cur, nxt
        has = {"tail": tail, "cur": cur, "next": nxt}
        order = [FILL_AT[s] for s in sorted(FILL_AT) if has[FILL_AT[s][0]]]
        self.number = {(name, i): n for n, (_, name, i) in enumerate(order)}
        self.fills = len(order)
        full = len(FILL_AT)
        before = sum(1 for kind, _, _ in FILL_AT.values() if kind == "next")
        first = before + sum(1 for kind, _, _ in FILL_AT.values() if kind != "tail")
        if isinstance(b, int) and b < 1:
            self.base = (0, before)[b + 1]
        elif isinstance(b, int) and b == B:
            self.base = first + full * (B - 2) + full - before
        else:
            self.base = (b - 1) * full + first

    def fill(self, s):
        if s not in FILL_AT:
            return None
        kind, name, i = FILL_AT[s]
        return (name, i) if {"tail": self.tail, "cur": self.cur, "next": self.next}[kind] else None

    def made(self, name, i):
        return self.base + self.number[(name, i)] + 1


def over_batches(eng, run):
    run(Iteration(-1, tail=False, cur=False))
    run(Iteration(0, tail=False))
    with eng.Fori(1, B - 1) as b:
        run(Iteration(b))
    run(Iteration(B - 1, nxt=False))
    run(Iteration(B, cur=False, nxt=False))


def wait(eng, sem, value):
    if not (isinstance(value, int) and value <= 0):
        eng.wait_ge(sem, value)


def wait_apart(eng, sem, value, passed):
    eng.wait_ge(sem, value)
    eng.sem_inc(passed, 1)


class Chain:

    def __init__(self, eng, sem, before):
        self.eng, self.sem, self.n = eng, sem, before

    def __call__(self, ins):
        self.n = self.n + 1
        ins.then_inc(self.sem, 1)
        self.eng.wait_ge(self.sem, self.n)


def rows_of(lt):
    return min(P, L - lt * P)


def attention_and_routing(nc, keep, x, ctx_t, g_xattn, g_ffn, wq_t, wk_t, wv_t, wo_t, router_t,
                          out, routed, q_parts_dram, k_parts_dram):
    ident, tri, ones, seen, pad_row = keep["ident"], keep["tri"], keep["ones"], keep["seen"], keep["pad_row"]
    x_rows = x.rearrange("b (t p) c -> b p t c", p=P)
    out_rows = out[0:TOKENS, :].rearrange("(b t p) c -> b p t c", p=P, t=NT)
    ctx_rows = ctx_t.rearrange("b (k p) l -> b p k l", p=P)

    with ExitStack() as ctx:
        def sb(name, shape, dt=F32):
            return ctx.enter_context(nc.sbuf_tensor(name, shape, dt))

        def sem(name):
            return ctx.enter_context(nc.semaphore(name))

        k_stack = sb("k_stack", [P, G, GH, L], BF16)
        q_stack = sb("q_stack", [P, G, GH, N], BF16)
        probs = sb("probs", [P, RING, GH, N])
        vz = sb("vz", [P, RING, GH, 32])
        v_ones = sb("v_ones", [P, 2, LT, H, DH + 1])
        ctx_sb = sb("ctx_sb", [P, KC, L])
        x_in = sb("x_in", [P, NT, D])
        x_t = sb("x_t", [P, KC, N])
        x2 = sb("x2", [P, NT, D])
        routed_rows = sb("routed_rows", [P, 2, NT, ROW])
        parts = sb("parts", [P, 2, 3, N], BF16)
        resid = sb("resid", [P, 2, N])
        o_acc = sb("o_acc", [P, N])
        attn = sb("attn", [P, NT, D])
        attn_t = sb("attn_t", [P, KC, N])
        row_t = sb("row_t", [P, KC, N])
        wq_sb = sb("wq_sb", [P, KC, D])
        wk_sb = sb("wk_sb", [P, KC, D])
        wv_sb = sb("wv_sb", [P, KC, D])
        wo_sb = sb("wo_sb", [P, KC, D])
        router_sb = sb("router_sb", [P, KC, E])
        gx = sb("gx", [P, 1])
        gf = sb("gf", [P, 1])
        tgx = sb("tgx", [P, 1])
        tgf = sb("tgf", [P, 1])
        negmax = sb("negmax", [P, 4, 2])
        z = sb("z", [P, RING, GH])
        rz = sb("rz", [P, RING, GH])
        rden = sb("rden", [P, NT, GH])
        stats1 = sb("stats1", [P, NT, 6])
        mv1 = sb("mv1", [P, NT, 2])
        rstd1 = sb("rstd1", [P, 2, NT])
        stats2 = sb("stats2", [P, NT, 6])
        mv2 = sb("mv2", [P, NT, 2])
        rstd2 = sb("rstd2", [P, 2, NT])
        minus_half = sb("minus_half", [P, NT])
        prob = sb("prob", [P, 3, NT, E])
        one_hot = sb("one_hot", [P, 2, NT, E])
        tmp = sb("tmp", [P, NT, E])
        top = sb("top", [P, 8, NT])
        chosen = sb("chosen", [P, NT, E])
        seen_at = sb("seen_at", [P, NT, E])
        slot = sb("slot", [P, NT, E])
        region_at = sb("region_at", [P, E])
        first_of = sb("first_of", [P, E])
        token = sb("token", [P, NT])
        place = sb("place", [P, 2, NT], U32)

        scores = ctx.enter_context(nc.psum_tensor("scores", [P, 2 * SLOTS, N], F32))
        acc = ctx.enter_context(nc.psum_tensor("acc", [P, N], F32))
        spare = ctx.enter_context(nc.psum_tensor("spare", [P, N], F32))

        weights_in = sem("weights_in")
        gates_in = sem("gates_in")
        constants = sem("constants")
        tanh_ready = sem("tanh_ready")
        dve_setup = sem("dve_setup")
        stack_in = [sem(f"stack_in_{g}") for g in range(G)]
        x_loaded = sem("x_loaded")
        ctx_loaded = sem("ctx_loaded")
        x2_loaded = sem("x2_loaded")
        scores_ready = sem("scores_ready")
        negmax_ready = sem("negmax_ready")
        exp_done = sem("exp_done")
        rz_ready = sem("rz_ready")
        vz_ready = sem("vz_ready")
        pv_done = sem("pv_done")
        acc_taken = sem("acc_taken")
        fill_ready = sem("fill_ready")
        fill_taken = sem("fill_taken")
        high_ready = sem("high_ready")
        middle_ready = sem("middle_ready")
        parts_ready = sem("parts_ready")
        parts_stored = [sem(f"parts_stored_{i}") for i in range(2)]
        stats_done = sem("stats_done")
        mv_ready = sem("mv_ready")
        rstd_step = sem("rstd_step")
        xn_ready = sem("xn_ready")
        rden_ready = sem("rden_ready")
        stats2_done = sem("stats2_done")
        mv2_ready = sem("mv2_ready")
        rstd2_step = sem("rstd2_step")
        rows_ready = sem("rows_ready")
        route_exp = sem("route_exp")
        route_step = sem("route_step")
        chosen_ready = sem("chosen_ready")
        place_step = sem("place_step")
        routed_out = sem("routed_out")
        x2_stored = sem("x2_stored")
        pads_stored = sem("pads_stored")

        passed_sp, passed_dve, passed_pool = (sem(f"passed_{e}") for e in ("sp", "dve", "pool"))
        PLACE_STEPS = 2 * 5 + 1

        block = ctx.enter_context(nc.Block())

        N_WEIGHTS = 5

        @block.sync
        def _(sp):
            for g_sb, g_in in ((gx, g_xattn), (gf, g_ffn)):
                sp.dma_start(g_sb[:, :], g_in.partition_broadcast(P)).then_inc(gates_in, 16)

            def run(it):
                b = it.b
                if it.next:
                    if it.cur:
                        wait_apart(sp, fill_taken, it.base, passed_sp)
                    sp.dma_start(x_in[:, :, :], x_rows[b + 1]).then_inc(x_loaded, 16)
                    sp.dma_start(ctx_sb[:, :, :], ctx_rows[b + 1]).then_inc(ctx_loaded, 16)
                    if isinstance(b, int) and b < 0:
                        for w_sb, w in ((wq_sb, wq_t), (wk_sb, wk_t), (wv_sb, wv_t), (wo_sb, wo_t), (router_sb, router_t)):
                            sp.dma_start(w_sb[:, :, :], w.rearrange("(k p) n -> p k n", p=P)).then_inc(weights_in, 16)
                if it.cur:
                    wait(sp, scores_ready, b * UNITS)
                    load_stacks(3)
                if it.tail:
                    sp.dma_start(x2[:, :, :], x_rows[b - 1]).then_inc(x2_loaded, 16)
                    sp.wait_ge(fill_taken, it.made("out_proj", 1))
                    sp.dma_start(out_rows[b - 1], x2[:, :, :]).then_inc(x2_stored, 16)
                if it.next:
                    if it.cur:
                        for g in range(G):
                            sp.wait_ge(stack_in[g], (b + 1) * LOADS)
                    for c in range(CHUNKS):
                        sp.wait_ge(parts_ready, (b + 1) * CHUNKS + c + 1)
                        if c < KC:
                            sp.dma_start(q_parts_dram[:, c * P:(c + 1) * P, :].rearrange("s p n -> p s n"),
                                         parts[:, c % 2, :, :]).then_inc(parts_stored[c % 2], 16)
                        else:
                            m, i = (c - KC) // KCHUNK, (c - KC) % KCHUNK
                            n = KCOLS[i + 1] - KCOLS[i]
                            sp.dma_start(k_parts_dram[:, m * P:(m + 1) * P, KCOLS[i]:KCOLS[i + 1]].rearrange("s p n -> p s n"),
                                         parts[:, c % 2, :, 0:n]).then_inc(parts_stored[c % 2], 16)
                    for half in range(2):
                        wait_apart(sp, parts_stored[half], (b + 2) * (CHUNKS // 2) * 16, passed_sp)
                    for g in range(G - 1):
                        if it.cur:
                            sp.wait_ge(scores_ready, b * UNITS + (g + 1) * 2 * LT)
                        load_stacks(g)
                if it.tail:
                    sp.wait_ge(x2_stored, b * 16)
                    wait_apart(sp, rows_ready, b, passed_sp)

            def load_stacks(g):
                for blk in range(BLOCKS):
                    rows = slice(blk * DH, (blk + 1) * DH)
                    heads = slice(g * GH * DH, (g + 1) * GH * DH)
                    sp.dma_start(q_stack[rows, g, :, :], q_parts_dram[Q_PART[blk], heads, :].rearrange(
                        "(h c) n -> c h n", c=DH)).then_inc(stack_in[g], 16)
                    sp.dma_start(k_stack[rows, g, :, :], k_parts_dram[K_PART[blk], heads, :].rearrange(
                        "(h c) n -> c h n", c=DH)).then_inc(stack_in[g], 16)

            over_batches(sp, run)

        @block.tensor
        def _(pe):
            pe.wait_ge(constants, 1)

            def fill(it, name, i):
                b = it.b
                wait(pe, fill_taken, it.made(name, i) - 1)
                if name == "x_turn":
                    pe.wait_ge(xn_ready, b + 2)
                    for t in range(NT):
                        mm = pe.transpose(spare[:, t * P:(t + 1) * P], x_in[:, t, i * P:(i + 1) * P], ident[:, :])
                elif name == "q":
                    if i == 0 and isinstance(b, int) and b < 0:
                        pe.wait_ge(weights_in, N_WEIGHTS * 16)
                    for k in range(KC):
                        mm = pe.matmul(spare[:, :], wq_sb[:, k, i * P:(i + 1) * P], x_t[:, k, :],
                                       start=(k == 0), stop=(k == KC - 1))
                elif name == "k":
                    if i == 0:
                        pe.wait_ge(ctx_loaded, (b + 2) * 16)
                    m, c = i // KCHUNK, i % KCHUNK
                    for k in range(KC):
                        mm = pe.matmul(spare[:, 0:KCOLS[c + 1] - KCOLS[c]], wk_sb[:, k, m * P:(m + 1) * P],
                                       ctx_sb[:, k, KCOLS[c]:KCOLS[c + 1]], start=(k == 0), stop=(k == KC - 1))
                elif name == "v":
                    for lt in range(2 * i, min(2 * i + 2, LT)):
                        r = rows_of(lt)
                        for k in range(KC):
                            mm = pe.matmul(spare[0:r, (lt % 2) * D:(lt % 2 + 1) * D], ctx_sb[:, k, lt * P:lt * P + r],
                                           wv_sb[:, k, :], start=(k == 0), stop=(k == KC - 1))
                elif name == "o_turn":
                    pe.wait_ge(acc_taken, b * G + i + 1 if i < G - 1 else b * G)
                    for t in range(NT):
                        mm = pe.transpose(spare[:, t * P:(t + 1) * P], o_acc[:, t * P:(t + 1) * P], ident[:, :])
                elif name == "attn_turn":
                    for t in range(NT):
                        mm = pe.transpose(spare[:, t * P:(t + 1) * P], attn[:, t, i * P:(i + 1) * P], ident[:, :])
                elif name == "out_proj":
                    for t in (2 * i, 2 * i + 1):
                        for k in range(KC):
                            mm = pe.matmul(spare[:, (t % 2) * D:(t % 2 + 1) * D], attn_t[:, k, t * P:(t + 1) * P],
                                           wo_sb[:, k, :], start=(k == 0), stop=(k == KC - 1))
                elif name == "row_turn":
                    pe.wait_ge(rows_ready, b)
                    for t in range(NT):
                        mm = pe.transpose(spare[:, t * P:(t + 1) * P], routed_rows[:, 0, t, i * P:(i + 1) * P], ident[:, :])
                elif name == "logits":
                    for t in range(NT):
                        for k in range(KC):
                            mm = pe.matmul(spare[:, t * E:(t + 1) * E], row_t[:, k, t * P:(t + 1) * P],
                                           router_sb[:, k, :], start=(k == 0), stop=(k == KC - 1))
                else:
                    pe.wait_ge(chosen_ready, b)
                    pe.matmul(spare[:, 0:NT * E], tri[:, :], chosen[:, :, :], start=True, stop=False)
                    mm = pe.matmul(spare[:, 0:NT * E], ones[:, :], seen_at[:, :, :], start=False, stop=True)
                mm.then_inc(fill_ready, 1)

            def unit_scores(b, s, p):
                u = 2 * s + p
                g, lt = s // LT, s % LT
                if lt == 0 and p == 0:
                    pe.wait_ge(stack_in[g], (b + 1) * LOADS)
                wait(pe, exp_done, b * UNITS + (u - SLOTS + 1 if u >= SLOTS else (-1, 0, -2)[u]))
                for j in (2 * p, 2 * p + 1):
                    r = rows_of(lt)
                    mm = pe.matmul(scores[0:r, 2 * (u % SLOTS) + j % 2, :], k_stack[:, g, j, lt * P:lt * P + r],
                                   q_stack[:, g, j, :], start=True, stop=True)
                mm.then_inc(scores_ready, 1)

            def weigh(b, s):
                lt = s % LT
                r = rows_of(lt)
                pe.wait_ge(vz_ready, b * STEPS + s + 1)
                if lt == 0:
                    wait(pe, acc_taken, b * G + s // LT)
                for j in range(GH):
                    mm = pe.matmul(acc[32 * j:32 * j + 32, :], vz[0:r, s % RING, j, :], probs[0:r, s % RING, j, :],
                                   start=(lt == 0), stop=(lt == LT - 1))
                mm.then_inc(pv_done, 1)

            def run(it):
                for s in range(STEPS):
                    if it.cur:
                        unit_scores(it.b, s, 0)
                    if it.fill(s):
                        fill(it, *it.fill(s))
                    if it.cur:
                        unit_scores(it.b, s, 1)
                    if s >= 2 and it.cur:
                        weigh(it.b, s - 2)
                    if s < 2 and it.tail:
                        weigh(it.b - 1, STEPS + s - 2)

            over_batches(pe, run)

        @block.scalar
        def _(act):
            act.wait_ge(gates_in, 32)
            act.activation(tgx[:, :], gx[:, :], ACT.Tanh).then_inc(tanh_ready, 1)
            act.activation(tgf[:, :], gf[:, :], ACT.Tanh).then_inc(tanh_ready, 1)

            def take(it, name, i):
                b = it.b
                if name in ("q", "k"):
                    c = i if name == "q" else KC + i
                    n = N if name == "q" else KCOLS[i % KCHUNK + 1] - KCOLS[i % KCHUNK]
                    act.wait_ge(fill_ready, it.made(name, i))
                    wait(act, parts_stored[c % 2], ((b + 1) * (CHUNKS // 2) + c // 2) * 16)
                    act.activation(parts[:, c % 2, 0, 0:n], spare[:, 0:n], ACT.Copy,
                                   scale=D ** -0.5 if name == "q" else 1.0).then_inc(high_ready, 1)
                elif name == "v":
                    act.wait_ge(fill_ready, it.made(name, i))
                    if i == 0 and (not isinstance(b, int) or b > 0):
                        act.wait_ge(vz_ready, b * STEPS)
                    m = min(2, LT - 2 * i)
                    r = rows_of(2 * i) if m == 1 else P
                    act.copy(v_ones[0:r, (b + 1) % 2, 2 * i:2 * i + m, :, 0:DH],
                             spare[0:r, 0:m * D].rearrange("p (t h c) -> p t h c", t=m, h=H)).then_inc(fill_taken, 1)
                elif name == "logits":
                    act.wait_ge(fill_taken, it.made("logits", 0))
                    act.activation(prob[:, 1, :, :], prob[:, 0, :, :], ACT.Exp).then_inc(route_exp, 1)

            def run(it):
                b = it.b
                for s in range(STEPS):
                    if it.fill(s) and it.fill(s)[0] != "logits":
                        take(it, *it.fill(s))
                    if s > 0 and it.fill(s - 1) and it.fill(s - 1)[0] == "logits":
                        take(it, "logits", 0)
                    if not it.cur:
                        continue
                    for p in range(2):
                        u = 2 * s + p
                        lt = s % LT
                        r = rows_of(lt)
                        act.wait_ge(negmax_ready, b * UNITS + u + 1)
                        if p == 0:
                            wait(act, pv_done, b * STEPS + s - RING + 1)
                        for j in (2 * p, 2 * p + 1):
                            e = act.activation(probs[0:r, s % RING, j, :], scores[0:r, 2 * (u % SLOTS) + j % 2, :],
                                               ACT.Exp, bias=negmax[0:r, u % 4, j % 2:j % 2 + 1],
                                               accum_out=z[0:r, s % RING, j:j + 1])
                        e.then_inc(exp_done, 1)

            over_batches(act, run)

        @block.vector
        def _(dve):
            dve.memset(vz[:, :, :, :], 0.0)
            dve.memset(v_ones[:, :, :, :, :], 1.0)
            dve.memset(minus_half[:, :], -0.5)
            dve.memset(seen[:, :], 0.0).then_inc(dve_setup, 1)
            for e in range(E):
                dve.memset(region_at[:, e:e + 1], float(e * REGION))
                dve.memset(first_of[:, e:e + 1], float(E - e))
            dve.wait_ge(tanh_ready, 2)
            dve.wait_ge(constants, 1)

            def bc(ap):
                return ap.unsqueeze(2).to_broadcast([P, NT, E])

            def pick(chain, k, values, free):
                chain(dve.tensor_reduce(top[:, k, :], values, AX.X, ALU.max))
                chain(dve.tensor_tensor(tmp[:, :, :], values, bc(top[:, k, :]), ALU.is_equal))
                chain(dve.tensor_tensor(tmp[:, :, :], tmp[:, :, :],
                                        first_of[:, :].unsqueeze(1).to_broadcast([P, NT, E]), ALU.mult))
                chain(dve.tensor_reduce(top[:, free, :], tmp[:, :, :], AX.X, ALU.max))
                chain(dve.tensor_tensor(one_hot[:, k, :, :], tmp[:, :, :], bc(top[:, free, :]), ALU.is_equal))

            def take(it, name, i):
                b = it.b
                dve.wait_ge(fill_ready, it.made(name, i))
                if name in ("x_turn", "attn_turn", "row_turn"):
                    to = {"x_turn": x_t, "attn_turn": attn_t, "row_turn": row_t}[name]
                    dve.tensor_copy(to[:, i, :], spare[:, :]).then_inc(fill_taken, 1)
                elif name in ("q", "k"):
                    c = i if name == "q" else KC + i
                    n = N if name == "q" else KCOLS[i % KCHUNK + 1] - KCOLS[i % KCHUNK]
                    dve.wait_ge(high_ready, (b + 1) * CHUNKS + c + 1)
                    dve.scalar_tensor_tensor(out=resid[:, c % 2, 0:n], in0=spare[:, 0:n],
                                             scalar=D ** -0.5 if name == "q" else 1.0, in1=parts[:, c % 2, 0, 0:n],
                                             op0=ALU.mult, op1=ALU.subtract).then_inc(fill_taken, 1)
                elif name == "o_turn":
                    of = spare[:, :].rearrange("p (t j c) -> p t j c", t=NT, j=GH)
                    dve.reciprocal(rden[:, :, :], of[:, :, :, DH]).then_inc(rden_ready, 1)
                    dve.wait_ge(rden_ready, b * G + i + 1 if i < G - 1 else b * G)
                    dve.tensor_tensor(attn[:, :, i * GH * DH:(i + 1) * GH * DH].rearrange("p t (j c) -> p t j c", j=GH),
                                      of[:, :, :, 0:DH], rden[:, :, :].unsqueeze(3).to_broadcast([P, NT, GH, DH]),
                                      ALU.mult).then_inc(fill_taken, 1)
                elif name == "out_proj":
                    if i == 0:
                        dve.wait_ge(x2_loaded, b * 16)
                    view = x2[:, 2 * i:2 * i + 2, :].rearrange("p t c -> p (t c)")
                    dve.scalar_tensor_tensor(out=view, in0=spare[:, :], scalar=tgx[:, 0:1], in1=view,
                                             op0=ALU.mult, op1=ALU.add).then_inc(fill_taken, 1)
                elif name == "logits":
                    lg = spare[:, 0:NT * E].rearrange("p (t e) -> p t e", t=NT)
                    chain = Chain(dve, route_step, (b - 1) * ROUTE_STEPS)
                    chain(dve.tensor_reduce(top[:, 7, :], lg, AX.X, ALU.max))
                    dve.tensor_tensor(prob[:, 0, :, :], lg, bc(top[:, 7, :]), ALU.subtract).then_inc(fill_taken, 1)
                elif name == "prefix":
                    chain = Chain(dve, place_step, (b - 1) * PLACE_STEPS)
                    dve.tensor_tensor(slot[:, :, :], spare[:, 0:NT * E].rearrange("p (t e) -> p t e", t=NT),
                                      region_at[:, :].unsqueeze(1).to_broadcast([P, NT, E]), ALU.add).then_inc(fill_taken, 1)
                    dve.wait_ge(fill_taken, it.made("prefix", 0))
                    for k in range(2):
                        chain(dve.tensor_tensor(tmp[:, :, :], slot[:, :, :], one_hot[:, k, :, :], ALU.mult))
                        chain(dve.tensor_reduce(top[:, 6, :], tmp[:, :, :], AX.X, ALU.add))
                        chain(dve.tensor_copy(place[:, k, :], top[:, 6, :]))
                        chain(dve.tensor_copy(routed_rows[:, k, :, D].unsqueeze(2), top[:, 4 + k, :].unsqueeze(2)))
                        chain(dve.tensor_copy(routed_rows[:, k, :, D + 1].bitcast(U32).unsqueeze(2), token[:, :].unsqueeze(2)))
                    chain(dve.tensor_scalar(token[:, :], token[:, :], float(N), None, ALU.add))

            def route(b):
                dve.wait_ge(route_exp, b)
                chain = Chain(dve, route_step, (b - 1) * ROUTE_STEPS + 1)
                chain(dve.tensor_reduce(top[:, 6, :], prob[:, 1, :, :], AX.X, ALU.add))
                chain(dve.reciprocal(top[:, 7, :], top[:, 6, :]))
                chain(dve.tensor_tensor(prob[:, 0, :, :], prob[:, 1, :, :], bc(top[:, 7, :]), ALU.mult))
                pick(chain, 0, prob[:, 0, :, :], 2)
                chain(dve.tensor_scalar(tmp[:, :, :], one_hot[:, 0, :, :], -2.0, None, ALU.mult))
                chain(dve.tensor_tensor(prob[:, 2, :, :], prob[:, 0, :, :], tmp[:, :, :], ALU.add))
                pick(chain, 1, prob[:, 2, :, :], 3)
                chain(dve.tensor_tensor(top[:, 6, :], top[:, 0, :], top[:, 1, :], ALU.add))
                chain(dve.reciprocal(top[:, 7, :], top[:, 6, :]))
                chain(dve.tensor_scalar(top[:, 7, :], top[:, 7, :], tgf[:, 0:1], None, ALU.mult))
                for k in range(2):
                    chain(dve.tensor_tensor(top[:, 4 + k, :], top[:, k, :], top[:, 7, :], ALU.mult))
                chain(dve.tensor_tensor(chosen[:, :, :], one_hot[:, 0, :, :], one_hot[:, 1, :, :], ALU.add))
                chain(dve.tensor_copy(seen_at[:, 0, :], seen[:, :]))
                for t in range(1, NT):
                    chain(dve.tensor_tensor(seen_at[:, t, :], seen_at[:, t - 1, :], chosen[:, t - 1, :], ALU.add))
                dve.tensor_tensor(seen[:, :], seen_at[:, NT - 1, :], chosen[:, NT - 1, :], ALU.add).then_inc(chosen_ready, 1)
                dve.wait_ge(chosen_ready, b)

            ROUTE_STEPS = 1 + 3 + 5 + 2 + 5 + 3 + 2 + 1 + 1 + (NT - 1)

            def reciprocals(b, s):
                r = rows_of(s % LT)
                dve.wait_ge(exp_done, b * UNITS + 2 * s + 2)
                dve.reciprocal(rz[0:r, s % RING, :], z[0:r, s % RING, :]).then_inc(rz_ready, 1)

            def take_acc(b, g):
                dve.wait_ge(pv_done, b * STEPS + (g + 1) * LT)
                dve.tensor_copy(o_acc[:, :], acc[:, :]).then_inc(acc_taken, 1)

            def run(it):
                b = it.b
                for s in range(STEPS):
                    for p in range(2):
                        if it.cur:
                            u = 2 * s + p
                            r = rows_of(s % LT)
                            dve.wait_ge(scores_ready, b * UNITS + u + 1)
                            dve.tensor_reduce(negmax[0:r, u % 4, :], scores[0:r, 2 * (u % SLOTS):2 * (u % SLOTS) + 2, :],
                                              AX.X, ALU.max, negate=True).then_inc(negmax_ready, 1)
                        if p == 0 and s == 2 and it.tail:
                            take_acc(b - 1, G - 1)
                        if p == 0 and it.cur and s in (LT + 2, 2 * LT + 2, 3 * LT + 2):
                            take_acc(b, s // LT - 1)
                        if p == 1 and s == 0 and it.tail:
                            reciprocals(b - 1, STEPS - 1)
                        if p == 1 and s > 0 and it.cur:
                            reciprocals(b, s - 1)
                        f = it.fill(s)
                        if f and f[0] != "v" and p == (f[0] in ("q", "k")):
                            take(it, *f)
                        if p == 1 and it.next and 2 <= s < 2 + NT:
                            t = s - 2
                            if t == 0:
                                dve.wait_ge(x_loaded, (b + 2) * 16)
                            dve.bn_stats(stats1[:, t, :], x_in[:, t, :]).then_inc(stats_done, 1)
                        if p == 1 and it.next and s == 6:
                            wait_apart(dve, stats_done, (b + 2) * NT, passed_dve)
                            for t in range(NT):
                                dve.bn_aggr(mv1[:, t, :], stats1[:, t, :]).then_inc(mv_ready, 1)
                        if p == 1 and it.tail and s == 7:
                            dve.wait_ge(fill_taken, it.made("out_proj", 1))
                        if p == 1 and it.tail and s in (7, 8):
                            for t in range(2 * (s - 7), 2 * (s - 7) + 2):
                                dve.bn_stats(stats2[:, t, :], x2[:, t, :]).then_inc(stats2_done, 1)
                        if p == 0 and it.tail and s == 9:
                            wait_apart(dve, stats2_done, b * NT, passed_dve)
                            for t in range(NT):
                                dve.bn_aggr(mv2[:, t, :], stats2[:, t, :]).then_inc(mv2_ready, 1)
                        if p == 0 and it.tail and s == 15:
                            route(b)

            dve.wait_ge(dve_setup, 1)
            dve.wait_ge(dve_setup, 1)
            dve.drain().then_inc(dve_setup, 1)
            dve.wait_ge(dve_setup, 2)
            over_batches(dve, run)

        @block.gpsimd
        def _(pool):
            pool.memset(ident[:, :], 0.0).then_inc(keep["built"], 1)
            pool.memset(tri[:, :], 1.0).then_inc(keep["built"], 1)
            pool.memset(ones[:, :], 1.0).then_inc(keep["built"], 1)
            pool.memset(pad_row[:, 0:D + 1], 0.0).then_inc(keep["built"], 1)
            pool.iota(token[:, :], pattern=[[P, NT]], base=0, channel_multiplier=1,
                      allow_small_or_imprecise_dtypes=True).then_inc(keep["built"], 1)
            pool.iota(pad_row[:, D + 1:D + 2].bitcast(U32), pattern=[[0, 1]], base=TOKENS,
                      channel_multiplier=1).then_inc(keep["built"], 1)
            pool.wait_ge(keep["built"], 6)
            pool.affine_select(out=ident[:, :], in_=ident[:, :], compare_op=ALU.not_equal, fill=1.0, base=0,
                               pattern=[[-1, P]], channel_multiplier=1).then_inc(keep["built"], 1)
            pool.affine_select(out=tri[:, :], in_=tri[:, :], compare_op=ALU.is_gt, fill=0.0, base=0,
                               pattern=[[1, P]], channel_multiplier=-1).then_inc(keep["built"], 1)
            pool.wait_ge(keep["built"], 8)
            pool.drain().then_inc(constants, 1)
            pool.dma_start(out[TOKENS:TOKENS + P, :], pad_row[:, 0:D]).then_inc(pads_stored, 16)
            pool.wait_ge(dve_setup, 2)

            def normalise(mv, rstd, step, before, src, dsts, ready):
                pool.tensor_scalar(rstd[:, 0, :], mv[:, :, 1], EPS, None, ALU.add).then_inc(step, 1)
                pool.wait_ge(step, before + 1)
                pool.tensor_tensor(rstd[:, 1, :], rstd[:, 0, :], minus_half[:, :], ALU.pow).then_inc(step, 1)
                wait_apart(pool, step, before + 2, passed_pool)
                for dst in dsts:
                    for t in range(NT):
                        ins = pool.tensor_scalar(dst[:, t, 0:D], src[:, t, :], mv[:, t, 0:1], rstd[:, 1, t:t + 1],
                                                 ALU.subtract, ALU.mult)
                ins.then_inc(ready, 1)

            def weigh_values(b, s):
                g, lt = s // LT, s % LT
                r = rows_of(lt)
                pool.wait_ge(rz_ready, b * STEPS + s + 1)
                wait(pool, pv_done, b * STEPS + s - RING + 1)
                pool.tensor_tensor(vz[0:r, s % RING, :, 0:DH + 1], v_ones[0:r, b % 2, lt, g * GH:(g + 1) * GH, :],
                                   rz[0:r, s % RING, :].unsqueeze(2).to_broadcast([r, GH, DH + 1]),
                                   ALU.mult).then_inc(vz_ready, 1)

            def run(it):
                b = it.b
                for s in range(STEPS):
                    if s == 0 and it.cur:
                        pool.wait_ge(fill_taken, it.base)
                    if it.cur and s >= 1:
                        weigh_values(b, s - 1)
                    if it.tail and s == 0:
                        weigh_values(b - 1, STEPS - 1)
                    if it.next and s == 7:
                        wait_apart(pool, mv_ready, (b + 2) * NT, passed_pool)
                        normalise(mv1, rstd1, rstd_step, (b + 1) * 2, x_in, [x_in], xn_ready)
                    if it.tail and s == 9:
                        wait_apart(pool, mv2_ready, b * NT, passed_pool)
                        normalise(mv2, rstd2, rstd2_step, (b - 1) * 2, x2,
                                  [routed_rows[:, 1, :, :], routed_rows[:, 0, :, :]], rows_ready)
                    f = it.fill(s)
                    if f and f[0] in ("q", "k"):
                        name, i = f
                        c = i if name == "q" else KC + i
                        n = N if name == "q" else KCOLS[i % KCHUNK + 1] - KCOLS[i % KCHUNK]
                        wait_apart(pool, fill_taken, it.made(name, i), passed_pool)
                        pool.tensor_copy(parts[:, c % 2, 1, 0:n], resid[:, c % 2, 0:n]).then_inc(middle_ready, 1)
                        pool.wait_ge(middle_ready, (b + 1) * CHUNKS + c + 1)
                        pool.tensor_tensor(parts[:, c % 2, 2, 0:n], resid[:, c % 2, 0:n], parts[:, c % 2, 1, 0:n],
                                           ALU.subtract).then_inc(parts_ready, 1)
                    if it.tail and 21 <= s < 21 + 2 * NT:
                        k, t = (s - 21) // NT, (s - 21) % NT
                        if s == 21:
                            wait_apart(pool, place_step, b * PLACE_STEPS, passed_pool)
                        pool.indirect_dma_start(
                            out=routed, out_offset=bass.IndirectOffsetOnAxis(place[:, k, t:t + 1], 0),
                            in_=routed_rows[:, k, t, :], in_offset=None).then_inc(routed_out, 16)
                    if it.tail and s == STEPS - 5:
                        pool.wait_ge(routed_out, b * 2 * NT * 16)

            over_batches(pool, run)
            pool.wait_ge(pads_stored, 16)


def experts(nc, keep, w1, w2, routed, out):
    ident, ones, seen, pad_row = keep["ident"], keep["ones"], keep["seen"], keep["pad_row"]
    HC = HID // P
    HB = BLK // P
    w1_rows = w1.rearrange("e (k p) h -> e p k h", p=P)
    w2_rows = w2.rearrange("e (k p) c -> e p k c", p=P)
    MIDDLE = NBLK - 5
    assert MIDDLE % 2 == 0

    with ExitStack() as ctx:
        def sb(name, shape, dt=F32):
            return ctx.enter_context(nc.sbuf_tensor(name, shape, dt))

        def psum(name, shape):
            return ctx.enter_context(nc.psum_tensor(name, shape, F32))

        def sem(name):
            return ctx.enter_context(nc.semaphore(name))

        rows = sb("rows", [P, 2, HB, ROW])
        w1_sb = sb("w1_sb", [P, 2, KC, HID])
        w2_sb = sb("w2_sb", [P, 2, HC, D])
        rows_t = sb("rows_t", [P, 2, KC, BLK])
        hidden = sb("hidden", [P, 2, HC, BLK])
        gate_token = sb("gate_token", [P, 2, HB, 2])
        result = sb("result", [P, 2, HB, D])
        count = sb("count", [P, E])
        count_up = sb("count_up", [P, E], I32)
        blocks_i = sb("blocks_i", [P, E], I32)
        blocks_of = sb("blocks_of", [P, E])
        ones_e = sb("ones_e", [P, E])
        last_of = sb("last_of", [P, E])
        region_of = sb("region_of", [P, E])
        pad_at = sb("pad_at", [P, E])
        number = sb("number", [P, NBLK])
        past = sb("past", [P, NBLK, E])
        expert_f = sb("expert_f", [P, NBLK])
        first_f = sb("first_f", [P, NBLK])
        row_f = sb("row_f", [P, NBLK])
        plan = sb("plan", [P, 3, NBLK], I32)

        ps_count = psum("ps_count", [P, 512])
        ps_rows = psum("ps_rows", [P, 512])
        ps_hidden = psum("ps_hidden", [P, 4, 512])
        ps_y = psum("ps_y", [P, 2, 512])

        numbers = sem("numbers")
        counted = sem("counted")
        plan_step = sem("plan_step")
        plan_ready = sem("plan_ready")
        pads_in = sem("pads_in")
        rows_in = [sem(f"rows_in_{slot}") for slot in range(2)]
        w1_in = [sem(f"w1_in_{slot}") for slot in range(2)]
        w2_in = [sem(f"w2_in_{slot}") for slot in range(2)]
        turned = sem("turned")
        rows_taken = sem("rows_taken")
        gates_taken = sem("gates_taken")
        hidden_ready = sem("hidden_ready")
        gelu_done = sem("gelu_done")
        y_ready = sem("y_ready")
        scaled = sem("scaled")
        added = sem("added")
        passed_pool = sem("passed_in_experts")

        block = ctx.enter_context(nc.Block())

        def over_blocks(eng, run):
            run(1, 1, False)
            run(2, 0, False)
            with eng.Fori(0, MIDDLE // 2) as i:
                run(i * 2 + 3, 1, False)
                run(i * 2 + 4, 0, False)
            run(NBLK - 2, (NBLK - 2) % 2, False)
            run(NBLK - 1, (NBLK - 1) % 2, True)

        @block.sync
        def _(sp):
            sp.wait_ge(plan_ready, 1)
            with sp.Fori(0, E) as e:
                at = nc.values_load(plan[0:1, 2, bass.ds(e, 1)], engines=[SP_ENGINE], min_val=0, max_val=SPARE)
                for half in range(HB):
                    sp.dma_start(routed[bass.ds(at + half * P, P), :], pad_row[:, :]).then_inc(pads_in, 16)
            for half in range(HB):
                sp.dma_start(routed[SPARE + half * P:SPARE + (half + 1) * P, :], pad_row[:, :]).then_inc(pads_in, 16)
            sp.wait_ge(pads_in, (E + 1) * HB * 16)

            def load(j, slot):
                e = nc.values_load(plan[0:1, 0, bass.ds(j, 1)], engines=[SP_ENGINE], min_val=0, max_val=E - 1)
                at = nc.values_load(plan[0:1, 1, bass.ds(j, 1)], engines=[SP_ENGINE], min_val=0, max_val=SPARE)
                wait(sp, rows_taken, j - 1)
                wait(sp, gates_taken, j - 1)
                sp.dma_start(rows[:, slot, :, :], routed[bass.ds(at, BLK), :].rearrange("(h p) c -> p h c", p=P)).then_inc(rows_in[slot], 16)
                wait(sp, y_ready, (j - 1) * HB)
                sp.dma_start(w1_sb[:, slot, :, :], w1_rows[e]).then_inc(w1_in[slot], 16)
                sp.dma_start(w2_sb[:, slot, :, :], w2_rows[e]).then_inc(w2_in[slot], 16)

            load(0, 0)
            load(1, 1)
            with sp.Fori(0, (NBLK - 3) // 2) as i:
                load(i * 2 + 2, 0)
                load(i * 2 + 3, 1)
            load(NBLK - 1, (NBLK - 1) % 2)

        @block.tensor
        def _(pe):
            pe.wait_ge(numbers, 1)
            pe.matmul(ps_count[:, 0:E], ones[:, :], seen[:, :], start=True, stop=True).then_inc(counted, 1)

            def turn(j, slot):
                pe.wait_ge(rows_in[slot], (j // 2 + 1) * 16)
                wait(pe, rows_taken, j)
                for k in range(KC):
                    for half in range(HB):
                        mm = pe.transpose(ps_rows[:, (k * HB + half) * P:(k * HB + half + 1) * P],
                                          rows[:, slot, half, k * P:(k + 1) * P], ident[:, :])
                mm.then_inc(turned, 1)

            def first(j, slot):
                pe.wait_ge(rows_taken, j + 1)
                pe.wait_ge(w1_in[slot], (j // 2 + 1) * 16)
                for h in range(HC):
                    if h % 2 == 0:
                        wait(pe, gelu_done, (j - 1) * (HC // 2) + h // 2 + 1)
                    for k in range(KC):
                        mm = pe.matmul(ps_hidden[:, h // 2, (h % 2) * BLK:(h % 2 + 1) * BLK],
                                       w1_sb[:, slot, k, h * P:(h + 1) * P], rows_t[:, slot, k, :],
                                       start=(k == 0), stop=(k == KC - 1))
                    if h % 2:
                        mm.then_inc(hidden_ready, 1)

            def second(j, slot, half):
                if half == 0:
                    pe.wait_ge(w2_in[slot], (j // 2 + 1) * 16)
                    pe.wait_ge(gelu_done, (j + 1) * (HC // 2))
                    wait(pe, scaled, (j - 1) * HB)
                for h in range(HC):
                    mm = pe.matmul(ps_y[:, slot, half * D:(half + 1) * D], hidden[:, slot, h, half * P:(half + 1) * P],
                                   w2_sb[:, slot, h, :], start=(h == 0), stop=(h == HC - 1))
                mm.then_inc(y_ready, 1)

            def run(j, slot, last):
                first(j, slot)
                second(j - 1, 1 - slot, 0)
                if not last:
                    turn(j + 1, 1 - slot)
                second(j - 1, 1 - slot, 1)

            turn(0, 0)
            first(0, 0)
            turn(1, 1)
            over_blocks(pe, run)
            for half in range(HB):
                second(NBLK - 1, (NBLK - 1) % 2, half)

        @block.scalar
        def _(act):
            def run(j, slot, last):
                for q in range(HC // 2):
                    act.wait_ge(hidden_ready, j * (HC // 2) + q + 1)
                    if q == 0:
                        wait(act, y_ready, (j - 1) * HB)
                    act.activation(hidden[:, slot, 2 * q:2 * q + 2, :].rearrange("p h n -> p (h n)"), ps_hidden[:, q, :],
                                   ACT.Gelu).then_inc(gelu_done, 1)

            run(0, 0, False)
            over_blocks(act, run)

        @block.vector
        def _(dve):
            chain = Chain(dve, plan_step, 0)
            chain(dve.memset(ones_e[:, :], 1.0))
            for e in range(E):
                chain(dve.memset(region_of[:, e:e + 1], float(e * REGION)))
            dve.wait_ge(numbers, 1)
            dve.wait_ge(counted, 1)
            chain(dve.tensor_copy(count[:, :], ps_count[:, 0:E]))
            chain(dve.tensor_scalar(count_up[:, :], count[:, :], float(BLK - 1), None, ALU.add))
            chain(dve.tensor_scalar(blocks_i[:, :], count_up[:, :], BLK.bit_length() - 1, None, ALU.logical_shift_right))
            chain(dve.tensor_copy(blocks_of[:, :], blocks_i[:, :]))
            chain(dve.tensor_tensor_scan(last_of[:, :], ones_e[:, :], blocks_of[:, :], 0.0, ALU.mult, ALU.add))
            chain(dve.tensor_tensor(past[:, :, :], number[:, :].unsqueeze(2).to_broadcast([P, NBLK, E]),
                                    last_of[:, :].unsqueeze(1).to_broadcast([P, NBLK, E]), ALU.is_ge))
            chain(dve.tensor_reduce(expert_f[:, :], past[:, :, :], AX.X, ALU.add))
            chain(dve.tensor_tensor(past[:, :, :], past[:, :, :],
                                    blocks_of[:, :].unsqueeze(1).to_broadcast([P, NBLK, E]), ALU.mult))
            chain(dve.tensor_reduce(first_f[:, :], past[:, :, :], AX.X, ALU.add))
            chain(dve.tensor_tensor(row_f[:, :], number[:, :], first_f[:, :], ALU.subtract))
            chain(dve.tensor_scalar(row_f[:, :], row_f[:, :], float(BLK), None, ALU.mult))
            chain(dve.tensor_scalar(first_f[:, :], expert_f[:, :], float(REGION), None, ALU.mult))
            chain(dve.tensor_tensor(row_f[:, :], row_f[:, :], first_f[:, :], ALU.add))
            chain(dve.tensor_scalar(row_f[:, :], row_f[:, :], float(SPARE), None, ALU.min))
            chain(dve.tensor_scalar(expert_f[:, :], expert_f[:, :], float(E - 1), None, ALU.min))
            chain(dve.tensor_tensor(pad_at[:, :], count[:, :], region_of[:, :], ALU.add))
            chain(dve.tensor_copy(plan[:, 0, :], expert_f[:, :]))
            chain(dve.tensor_copy(plan[:, 1, :], row_f[:, :]))
            dve.tensor_copy(plan[:, 2, 0:E], pad_at[:, :]).then_inc(plan_ready, 1)

            def take_rows(j, slot):
                dve.wait_ge(turned, j + 1)
                dve.tensor_copy(rows_t[:, slot, :, :].rearrange("p k n -> p (k n)"), ps_rows[:, :]).then_inc(rows_taken, 1)

            def take_gates(j, slot):
                wait(dve, added, (j - 1) * HB * 16)
                dve.wait_ge(rows_in[slot], (j // 2 + 1) * 16)
                dve.tensor_copy(gate_token[:, slot, :, :], rows[:, slot, :, D:ROW]).then_inc(gates_taken, 1)

            def scale(j, slot, half):
                dve.wait_ge(y_ready, (j + 1) * HB)
                dve.tensor_scalar(result[:, slot, half, :], ps_y[:, slot, half * D:(half + 1) * D],
                                  gate_token[:, slot, half, 0:1], None, ALU.mult).then_inc(scaled, 1)

            def run(j, slot, last):
                if not last:
                    take_rows(j + 1, 1 - slot)
                for half in range(HB):
                    if half == 0:
                        dve.wait_ge(gates_taken, j)
                        wait(dve, added, (j - 2) * HB * 16)
                    scale(j - 1, 1 - slot, half)
                if not last:
                    take_gates(j + 1, 1 - slot)

            take_rows(0, 0)
            take_gates(0, 0)
            take_rows(1, 1)
            take_gates(1, 1)
            over_blocks(dve, run)
            for half in range(HB):
                if half == 0:
                    dve.wait_ge(gates_taken, NBLK)
                    wait(dve, added, (NBLK - 2) * HB * 16)
                scale(NBLK - 1, (NBLK - 1) % 2, half)

        @block.gpsimd
        def _(pool):
            pool.iota(number[:, :], pattern=[[1, NBLK]], base=0, channel_multiplier=0,
                      allow_small_or_imprecise_dtypes=True).then_inc(numbers, 1)

            def add(j, slot):
                for half in range(HB):
                    pool.wait_ge(scaled, j * HB + half + 1)
                    if not (isinstance(j, int) and j == 0 and half == 0):
                        wait_apart(pool, added, (j * HB + half) * 16, passed_pool)
                    pool.indirect_dma_start(
                        out=out, out_offset=bass.IndirectOffsetOnAxis(gate_token[:, slot, half, 1:2].bitcast(U32), 0),
                        in_=result[:, slot, half, :], in_offset=None, compute_op=ALU.add).then_inc(added, 16)

            add(0, 0)
            over_blocks(pool, lambda j, slot, last: add(j, slot))
            pool.wait_ge(added, NBLK * HB * 16)


def flamingo_block(nc, x, ctx_t, g_xattn, g_ffn, wq_t, wk_t, wv_t, wo_t, router_t, w1, w2, out):
    routed = nc.dram_tensor("routed", (SPARE + BLK, ROW), F32, kind="Internal").ap()
    q_parts_dram = nc.dram_tensor("q_parts", (3, D, N), BF16, kind="Internal").ap()
    k_parts_dram = nc.dram_tensor("k_parts", (3, D, L), BF16, kind="Internal").ap()
    with ExitStack() as ctx:
        keep = {name: ctx.enter_context(nc.sbuf_tensor(name, [P, n], F32))
                for name, n in (("ident", P), ("tri", P), ("ones", P), ("seen", E), ("pad_row", ROW))}
        keep["built"] = ctx.enter_context(nc.semaphore("built"))
        attention_and_routing(nc, keep, x, ctx_t, g_xattn, g_ffn, wq_t, wk_t, wv_t, wo_t, router_t,
                              out, routed, q_parts_dram, k_parts_dram)
        experts(nc, keep, w1, w2, routed, out)


def kernel(**inputs):
    import numpy as np
    import concourse.bacc as bacc
    from concourse.bass_utils import run_bass_kernel_spmd

    def turned(a):
        return np.ascontiguousarray(np.swapaxes(np.asarray(a), -1, -2))

    nc = bacc.Bacc("TRN2", target_bir_lowering=False, num_devices=1)
    given = [
        ("x", np.ascontiguousarray(inputs["x"])),
        ("ctx_t", turned(inputs["ctx_1024"])),
        ("g_xattn", np.ascontiguousarray(inputs["g_xattn"])),
        ("g_ffn", np.ascontiguousarray(inputs["g_ffn"])),
        ("wq_t", turned(inputs["L0_xattn_Wq"])),
        ("wk_t", turned(inputs["L0_xattn_Wk"])),
        ("wv_t", turned(inputs["L0_xattn_Wv"])),
        ("wo_t", turned(inputs["L0_xattn_Wo"])),
        ("router_t", turned(inputs["L0_ffn_router_w"])),
        ("w1", np.ascontiguousarray(inputs["L0_ffn_w1"])),
        ("w2", np.ascontiguousarray(inputs["L0_ffn_w2"])),
    ]
    arrays = {f"in_{name}": a for name, a in given}
    args = [nc.dram_tensor(f"in_{name}", a.shape, mybir.dt.from_np(a.dtype), kind="ExternalInput").ap()
            for name, a in given]
    out = nc.dram_tensor("out", (TOKENS + P, D), F32, kind="ExternalOutput").ap()
    flamingo_block(nc, *args, out)
    r = run_bass_kernel_spmd(nc, [arrays], core_ids=[0])
    return r.results[0]["out"][0:TOKENS].reshape(B, N, D)
```

```python
from contextlib import ExitStack

import concourse.bass as bass
from concourse import mybir

ALU = mybir.AluOpType
ACT = mybir.ActivationFunctionType
AX = mybir.AxisListType
F32 = mybir.dt.float32
BF16 = mybir.dt.bfloat16
I32 = mybir.dt.int32
U32 = mybir.dt.uint32
SP_ENGINE = mybir.EngineType.SP

P = 128
B, N, D = 8, 512, 256
L = 1601
H = 16
DH = D // H
E, HID = 8, 1024
EPS = 1e-5
KC = D // P
NT = N // P
LT = (L + P - 1) // P
GH = 4
G = H // GH
STEPS = G * LT
UNITS = 2 * STEPS
RING = 4
SLOTS = 3
K_PART = (0, 0, 0, 1, 1, 1, 2, 2)
Q_PART = (0, 1, 2, 0, 1, 2, 0, 1)
BLOCKS = len(K_PART)
KCHUNK = 4
KCOLS = [(L * i) // KCHUNK for i in range(KCHUNK + 1)]
KCMAX = max(KCOLS[i + 1] - KCOLS[i] for i in range(KCHUNK))
CHUNKS = KC + KC * KCHUNK
VF = (LT + 1) // 2
TOKENS = B * N
ROW = D + 2
BLK = 256
REGION = TOKENS + BLK
SPARE = E * REGION
NBLK = (2 * TOKENS) // BLK + E - 1
LOADS = 16 * 2 * BLOCKS

FILL_AT = {
    3: ("tail", "o_turn", 3), 4: ("tail", "attn_turn", 0), 5: ("tail", "attn_turn", 1),
    6: ("tail", "out_proj", 0), 7: ("tail", "out_proj", 1), 9: ("next", "v", 0), 11: ("next", "v", 1),
    13: ("next", "v", 2), 14: ("tail", "row_turn", 0), 15: ("next", "v", 3), 16: ("cur", "o_turn", 0),
    17: ("tail", "row_turn", 1), 19: ("tail", "logits", 0),
    20: ("next", "x_turn", 0), 21: ("next", "x_turn", 1), 22: ("next", "q", 0), 24: ("next", "q", 1),
    25: ("next", "k", 0), 27: ("next", "k", 1), 28: ("next", "k", 2), 29: ("cur", "o_turn", 1),
    30: ("next", "k", 3), 32: ("next", "k", 4), 34: ("next", "k", 5), 36: ("next", "k", 6),
    37: ("tail", "prefix", 0), 38: ("next", "k", 7), 40: ("next", "v", 4), 42: ("cur", "o_turn", 2),
    44: ("next", "v", 5), 47: ("next", "v", 6),
}


class Iteration:

    def __init__(self, b, tail=True, cur=True, nxt=True):
        self.b, self.tail, self.cur, self.next = b, tail, cur, nxt
        has = {"tail": tail, "cur": cur, "next": nxt}
        order = [FILL_AT[s] for s in sorted(FILL_AT) if has[FILL_AT[s][0]]]
        self.number = {(name, i): n for n, (_, name, i) in enumerate(order)}
        self.fills = len(order)
        full = len(FILL_AT)
        before = sum(1 for kind, _, _ in FILL_AT.values() if kind == "next")
        first = before + sum(1 for kind, _, _ in FILL_AT.values() if kind != "tail")
        if isinstance(b, int) and b < 1:
            self.base = (0, before)[b + 1]
        elif isinstance(b, int) and b == B:
            self.base = first + full * (B - 2) + full - before
        else:
            self.base = (b - 1) * full + first

    def fill(self, s):
        if s not in FILL_AT:
            return None
        kind, name, i = FILL_AT[s]
        return (name, i) if {"tail": self.tail, "cur": self.cur, "next": self.next}[kind] else None

    def made(self, name, i):
        return self.base + self.number[(name, i)] + 1


def over_batches(eng, run):
    run(Iteration(-1, tail=False, cur=False))
    run(Iteration(0, tail=False))
    with eng.Fori(1, B - 1) as b:
        run(Iteration(b))
    run(Iteration(B - 1, nxt=False))
    run(Iteration(B, cur=False, nxt=False))


def wait(eng, sem, value):
    if not (isinstance(value, int) and value <= 0):
        eng.wait_ge(sem, value)


def wait_apart(eng, sem, value, passed):
    eng.wait_ge(sem, value)
    eng.sem_inc(passed, 1)


class Chain:

    def __init__(self, eng, sem, before):
        self.eng, self.sem, self.n, self.any = eng, sem, before, False

    def __call__(self, ins):
        self.n, self.any = self.n + 1, True
        ins.then_inc(self.sem, 1)

    def settle(self):
        if self.any:
            self.eng.wait_ge(self.sem, self.n)


def in_turn(chain, steps):
    chain.settle()
    next(steps, None)


def rows_of(lt):
    return min(P, L - lt * P)


def attention_and_routing(nc, keep, x, ctx_t, g_xattn, g_ffn, wq_t, wk_t, wv_t, wo_t, router_t,
                          out, routed, q_parts_dram, k_parts_dram):
    ident, tri, ones, seen, pad_row = keep["ident"], keep["tri"], keep["ones"], keep["seen"], keep["pad_row"]
    x_rows = x.rearrange("b (t p) c -> b p t c", p=P)
    out_rows = out[0:TOKENS, :].rearrange("(b t p) c -> b p t c", p=P, t=NT)
    ctx_rows = ctx_t.rearrange("b (k p) l -> b p k l", p=P)

    with ExitStack() as ctx:
        def sb(name, shape, dt=F32):
            return ctx.enter_context(nc.sbuf_tensor(name, shape, dt))

        def sem(name):
            return ctx.enter_context(nc.semaphore(name))

        k_stack = sb("k_stack", [P, G, GH, L], BF16)
        q_stack = sb("q_stack", [P, G, GH, N], BF16)
        probs = sb("probs", [P, RING, GH, N])
        vz = sb("vz", [P, RING, GH, 32])
        v_ones = sb("v_ones", [P, 2, LT, H, DH + 1])
        ctx_sb = sb("ctx_sb", [P, KC, L])
        x_in = sb("x_in", [P, NT, D])
        x_t = sb("x_t", [P, KC, N])
        x2 = sb("x2", [P, NT, D])
        routed_rows = sb("routed_rows", [P, 2, NT, ROW])
        parts = sb("parts", [P, 2, 3, N], BF16)
        resid = sb("resid", [P, 2, N])
        o_acc = sb("o_acc", [P, N])
        attn = sb("attn", [P, NT, D])
        attn_t = sb("attn_t", [P, KC, N])
        row_t = sb("row_t", [P, KC, N])
        wq_sb = sb("wq_sb", [P, KC, D])
        wk_sb = sb("wk_sb", [P, KC, D])
        wv_sb = sb("wv_sb", [P, KC, D])
        wo_sb = sb("wo_sb", [P, KC, D])
        router_sb = sb("router_sb", [P, KC, E])
        gx = sb("gx", [P, 1])
        gf = sb("gf", [P, 1])
        tgx = sb("tgx", [P, 1])
        tgf = sb("tgf", [P, 1])
        negmax = sb("negmax", [P, 4, 2])
        z = sb("z", [P, RING, GH])
        rz = sb("rz", [P, RING, GH])
        rden = sb("rden", [P, NT, GH])
        stats1 = sb("stats1", [P, NT, 6])
        mv1 = sb("mv1", [P, NT, 2])
        rstd1 = sb("rstd1", [P, 2, NT])
        stats2 = sb("stats2", [P, NT, 6])
        mv2 = sb("mv2", [P, NT, 2])
        rstd2 = sb("rstd2", [P, 2, NT])
        minus_half = sb("minus_half", [P, NT])
        prob = sb("prob", [P, 3, NT, E])
        one_hot = sb("one_hot", [P, 2, NT, E])
        tmp = sb("tmp", [P, 2, NT, E])
        zero = sb("zero", [P, 1])
        top = sb("top", [P, 8, NT])
        chosen = sb("chosen", [P, NT, E])
        seen_at = sb("seen_at", [P, NT, E])
        slot = sb("slot", [P, NT, E])
        region_at = sb("region_at", [P, E])
        first_of = sb("first_of", [P, E])
        token = sb("token", [P, NT])
        place = sb("place", [P, 2, NT], U32)

        scores = ctx.enter_context(nc.psum_tensor("scores", [P, 2 * SLOTS, N], F32))
        acc = ctx.enter_context(nc.psum_tensor("acc", [P, N], F32))
        spare = ctx.enter_context(nc.psum_tensor("spare", [P, N], F32))

        weights_in = sem("weights_in")
        gates_in = sem("gates_in")
        constants = sem("constants")
        tanh_ready = sem("tanh_ready")
        dve_setup = sem("dve_setup")
        stack_in = [sem(f"stack_in_{g}") for g in range(G)]
        x_loaded = sem("x_loaded")
        ctx_loaded = sem("ctx_loaded")
        x2_loaded = sem("x2_loaded")
        scores_ready = sem("scores_ready")
        negmax_ready = sem("negmax_ready")
        exp_done = sem("exp_done")
        rz_ready = sem("rz_ready")
        vz_ready = sem("vz_ready")
        pv_done = sem("pv_done")
        acc_taken = sem("acc_taken")
        fill_ready = sem("fill_ready")
        fill_taken = sem("fill_taken")
        high_ready = sem("high_ready")
        middle_ready = sem("middle_ready")
        parts_ready = sem("parts_ready")
        parts_stored = [sem(f"parts_stored_{i}") for i in range(2)]
        stats_done = sem("stats_done")
        mv_ready = sem("mv_ready")
        rstd_step = sem("rstd_step")
        xn_ready = sem("xn_ready")
        rden_ready = sem("rden_ready")
        stats2_done = sem("stats2_done")
        mv2_ready = sem("mv2_ready")
        rstd2_step = sem("rstd2_step")
        rows_ready = sem("rows_ready")
        logits_max = sem("logits_max")
        route_exp = sem("route_exp")
        route_step = sem("route_step")
        place_step = sem("place_step")
        rows_out = sem("rows_out")
        x2_stored = sem("x2_stored")
        centred1 = sem("centred1")
        centred2 = sem("centred2")
        rows1_ready = sem("rows1_ready")

        passed_sp, passed_dve, passed_pool = (sem(f"passed_{e}") for e in ("sp", "dve", "pool"))
        ROUTE_STEPS, PLACE_STEPS = 25, 6
        DVE_SETUP = 5 + 2 * E

        block = ctx.enter_context(nc.Block())

        N_WEIGHTS = 5

        @block.sync
        def _(sp):
            for g_sb, g_in in ((gx, g_xattn), (gf, g_ffn)):
                sp.dma_start(g_sb[:, :], g_in.partition_broadcast(P)).then_inc(gates_in, 16)

            def run(it):
                b = it.b
                if it.next:
                    if it.cur:
                        wait_apart(sp, fill_taken, it.base, passed_sp)
                    sp.dma_start(x_in[:, :, :], x_rows[b + 1]).then_inc(x_loaded, 16)
                    sp.dma_start(ctx_sb[:, :, :], ctx_rows[b + 1]).then_inc(ctx_loaded, 16)
                    if isinstance(b, int) and b < 0:
                        for w_sb, w in ((wq_sb, wq_t), (wk_sb, wk_t), (wv_sb, wv_t), (wo_sb, wo_t), (router_sb, router_t)):
                            sp.dma_start(w_sb[:, :, :], w.rearrange("(k p) n -> p k n", p=P)).then_inc(weights_in, 16)
                if it.cur:
                    wait(sp, scores_ready, b * UNITS)
                    load_stacks(3)
                if it.tail:
                    sp.dma_start(x2[:, :, :], x_rows[b - 1]).then_inc(x2_loaded, 16)
                    sp.wait_ge(fill_taken, it.made("out_proj", 1))
                    sp.dma_start(out_rows[b - 1], x2[:, :, :]).then_inc(x2_stored, 16)
                if it.next:
                    if it.cur:
                        for g in range(G):
                            sp.wait_ge(stack_in[g], (b + 1) * LOADS)
                    for c in range(CHUNKS):
                        sp.wait_ge(parts_ready, (b + 1) * CHUNKS + c + 1)
                        if c < KC:
                            sp.dma_start(q_parts_dram[:, c * P:(c + 1) * P, :].rearrange("s p n -> p s n"),
                                         parts[:, c % 2, :, :]).then_inc(parts_stored[c % 2], 16)
                        else:
                            m, i = (c - KC) // KCHUNK, (c - KC) % KCHUNK
                            n = KCOLS[i + 1] - KCOLS[i]
                            sp.dma_start(k_parts_dram[:, m * P:(m + 1) * P, KCOLS[i]:KCOLS[i + 1]].rearrange("s p n -> p s n"),
                                         parts[:, c % 2, :, 0:n]).then_inc(parts_stored[c % 2], 16)
                    for half in range(2):
                        wait_apart(sp, parts_stored[half], (b + 2) * (CHUNKS // 2) * 16, passed_sp)
                    for g in range(G - 1):
                        if it.cur:
                            sp.wait_ge(scores_ready, b * UNITS + (g + 1) * 2 * LT)
                        load_stacks(g)
                if it.tail:
                    wait_apart(sp, x2_stored, b * 16, passed_sp)
                    wait_apart(sp, rows_ready, 2 * b, passed_sp)

            def load_stacks(g):
                for blk in range(BLOCKS):
                    rows = slice(blk * DH, (blk + 1) * DH)
                    heads = slice(g * GH * DH, (g + 1) * GH * DH)
                    sp.dma_start(q_stack[rows, g, :, :], q_parts_dram[Q_PART[blk], heads, :].rearrange(
                        "(h c) n -> c h n", c=DH)).then_inc(stack_in[g], 16)
                    sp.dma_start(k_stack[rows, g, :, :], k_parts_dram[K_PART[blk], heads, :].rearrange(
                        "(h c) n -> c h n", c=DH)).then_inc(stack_in[g], 16)

            over_batches(sp, run)

        @block.tensor
        def _(pe):
            pe.wait_ge(constants, 1)

            def fill(it, name, i):
                b = it.b
                wait(pe, fill_taken, it.made(name, i) - 1)
                if name == "x_turn":
                    pe.wait_ge(xn_ready, 2 * (b + 2))
                    for t in range(NT):
                        mm = pe.transpose(spare[:, t * P:(t + 1) * P], x_in[:, t, i * P:(i + 1) * P], ident[:, :])
                elif name == "q":
                    for k in range(KC):
                        mm = pe.matmul(spare[:, :], wq_sb[:, k, i * P:(i + 1) * P], x_t[:, k, :],
                                       start=(k == 0), stop=(k == KC - 1))
                elif name == "k":
                    m, c = i // KCHUNK, i % KCHUNK
                    for k in range(KC):
                        mm = pe.matmul(spare[:, 0:KCOLS[c + 1] - KCOLS[c]], wk_sb[:, k, m * P:(m + 1) * P],
                                       ctx_sb[:, k, KCOLS[c]:KCOLS[c + 1]], start=(k == 0), stop=(k == KC - 1))
                elif name == "v":
                    if i == 0:
                        if isinstance(b, int) and b < 0:
                            pe.wait_ge(weights_in, N_WEIGHTS * 16)
                        pe.wait_ge(ctx_loaded, (b + 2) * 16)
                    for lt in range(2 * i, min(2 * i + 2, LT)):
                        r = rows_of(lt)
                        for k in range(KC):
                            mm = pe.matmul(spare[0:r, (lt % 2) * D:(lt % 2 + 1) * D], ctx_sb[:, k, lt * P:lt * P + r],
                                           wv_sb[:, k, :], start=(k == 0), stop=(k == KC - 1))
                elif name == "o_turn":
                    pe.wait_ge(acc_taken, b * G + i + 1 if i < G - 1 else b * G)
                    for t in range(NT):
                        mm = pe.transpose(spare[:, t * P:(t + 1) * P], o_acc[:, t * P:(t + 1) * P], ident[:, :])
                elif name == "attn_turn":
                    for t in range(NT):
                        mm = pe.transpose(spare[:, t * P:(t + 1) * P], attn[:, t, i * P:(i + 1) * P], ident[:, :])
                elif name == "out_proj":
                    for t in (2 * i, 2 * i + 1):
                        for k in range(KC):
                            mm = pe.matmul(spare[:, (t % 2) * D:(t % 2 + 1) * D], attn_t[:, k, t * P:(t + 1) * P],
                                           wo_sb[:, k, :], start=(k == 0), stop=(k == KC - 1))
                elif name == "row_turn":
                    pe.wait_ge(rows_ready, 2 * b)
                    for t in range(NT):
                        mm = pe.transpose(spare[:, t * P:(t + 1) * P], routed_rows[:, 0, t, i * P:(i + 1) * P], ident[:, :])
                elif name == "logits":
                    for t in range(NT):
                        for k in range(KC):
                            mm = pe.matmul(spare[:, t * E:(t + 1) * E], row_t[:, k, t * P:(t + 1) * P],
                                           router_sb[:, k, :], start=(k == 0), stop=(k == KC - 1))
                else:
                    pe.wait_ge(route_step, b * ROUTE_STEPS)
                    pe.matmul(spare[:, 0:NT * E], tri[:, :], chosen[:, :, :], start=True, stop=False)
                    mm = pe.matmul(spare[:, 0:NT * E], ones[:, :], seen_at[:, :, :], start=False, stop=True)
                mm.then_inc(fill_ready, 1)

            def unit_scores(b, s, p):
                u = 2 * s + p
                g, lt = s // LT, s % LT
                if lt == 0 and p == 0:
                    pe.wait_ge(stack_in[g], (b + 1) * LOADS)
                wait(pe, exp_done, b * UNITS + (u - SLOTS + 1 if u >= SLOTS else (-1, 0, -2)[u]))
                for j in (2 * p, 2 * p + 1):
                    r = rows_of(lt)
                    mm = pe.matmul(scores[0:r, 2 * (u % SLOTS) + j % 2, :], k_stack[:, g, j, lt * P:lt * P + r],
                                   q_stack[:, g, j, :], start=True, stop=True)
                mm.then_inc(scores_ready, 1)

            def weigh(b, s):
                lt = s % LT
                r = rows_of(lt)
                pe.wait_ge(vz_ready, b * STEPS + s + 1)
                if lt == 0:
                    wait(pe, acc_taken, b * G + s // LT)
                for j in range(GH):
                    mm = pe.matmul(acc[32 * j:32 * j + 32, :], vz[0:r, s % RING, j, :], probs[0:r, s % RING, j, :],
                                   start=(lt == 0), stop=(lt == LT - 1))
                mm.then_inc(pv_done, 1)

            def run(it):
                for s in range(STEPS):
                    if it.cur:
                        unit_scores(it.b, s, 0)
                    if it.fill(s):
                        fill(it, *it.fill(s))
                    if it.cur:
                        unit_scores(it.b, s, 1)
                    if s >= 2 and it.cur:
                        weigh(it.b, s - 2)
                    if s < 2 and it.tail:
                        weigh(it.b - 1, STEPS + s - 2)

            over_batches(pe, run)

        @block.scalar
        def _(act):
            act.wait_ge(dve_setup, DVE_SETUP)
            act.wait_ge(gates_in, 32)
            act.activation(tgx[:, :], gx[:, :], ACT.Tanh).then_inc(tanh_ready, 1)
            act.activation(tgf[:, :], gf[:, :], ACT.Tanh).then_inc(tanh_ready, 1)

            def take(it, name, i):
                b = it.b
                if name in ("q", "k"):
                    c = i if name == "q" else KC + i
                    n = N if name == "q" else KCOLS[i % KCHUNK + 1] - KCOLS[i % KCHUNK]
                    act.wait_ge(fill_ready, it.made(name, i))
                    wait(act, parts_stored[c % 2], ((b + 1) * (CHUNKS // 2) + c // 2) * 16)
                    act.activation(parts[:, c % 2, 0, 0:n], spare[:, 0:n], ACT.Copy,
                                   scale=D ** -0.5 if name == "q" else 1.0).then_inc(high_ready, 1)
                elif name == "v":
                    act.wait_ge(fill_ready, it.made(name, i))
                    if i == 0 and (not isinstance(b, int) or b > 0):
                        act.wait_ge(vz_ready, b * STEPS)
                    m = min(2, LT - 2 * i)
                    r = rows_of(2 * i) if m == 1 else P
                    act.copy(v_ones[0:r, (b + 1) % 2, 2 * i:2 * i + m, :, 0:DH],
                             spare[0:r, 0:m * D].rearrange("p (t h c) -> p t h c", t=m, h=H)).then_inc(fill_taken, 1)
                elif name == "logits":
                    act.wait_ge(fill_taken, it.made("logits", 0))
                    act.activation(prob[:, 1, :, :], prob[:, 0, :, :], ACT.Exp).then_inc(route_exp, 1)

            def run(it):
                b = it.b
                for s in range(STEPS):
                    if it.fill(s) and it.fill(s)[0] != "logits":
                        take(it, *it.fill(s))
                    if s > 0 and it.fill(s - 1) and it.fill(s - 1)[0] == "logits":
                        take(it, "logits", 0)
                    if not it.cur:
                        continue
                    for p in range(2):
                        u = 2 * s + p
                        lt = s % LT
                        r = rows_of(lt)
                        act.wait_ge(negmax_ready, b * UNITS + u + 1)
                        if p == 0:
                            wait(act, pv_done, b * STEPS + s - RING + 1)
                        for j in (2 * p, 2 * p + 1):
                            e = act.activation(probs[0:r, s % RING, j, :], scores[0:r, 2 * (u % SLOTS) + j % 2, :],
                                               ACT.Exp, bias=negmax[0:r, u % 4, j % 2:j % 2 + 1],
                                               accum_out=z[0:r, s % RING, j:j + 1])
                        e.then_inc(exp_done, 1)

            over_batches(act, run)

        @block.vector
        def _(dve):
            for tile, value in ((v_ones[:, :, :, :, DH], 1.0), (vz[:, :, :, :], 0.0), (minus_half[:, :], -0.5),
                                (zero[:, :], 0.0), (seen[:, :], 0.0)):
                dve.memset(tile, value).then_inc(dve_setup, 1)
            for e in range(E):
                dve.memset(region_at[:, e:e + 1], float(e * REGION)).then_inc(dve_setup, 1)
                dve.memset(first_of[:, e:e + 1], float(E - e)).then_inc(dve_setup, 1)
            dve.wait_ge(dve_setup, DVE_SETUP)
            dve.wait_ge(tanh_ready, 2)
            dve.wait_ge(constants, 1)

            def bc(ap):
                return ap.unsqueeze(2).to_broadcast([P, NT, E])

            def pick(chain, k, values, free):
                chain(dve.tensor_reduce(top[:, k, :], values, AX.X, ALU.max))
                yield
                chain(dve.tensor_tensor(tmp[:, 0, :, :], values, bc(top[:, k, :]), ALU.is_equal))
                yield
                chain(dve.tensor_tensor(tmp[:, 0, :, :], tmp[:, 0, :, :],
                                        first_of[:, :].unsqueeze(1).to_broadcast([P, NT, E]), ALU.mult))
                yield
                chain(dve.tensor_reduce(top[:, free, :], tmp[:, 0, :, :], AX.X, ALU.max))
                yield
                chain(dve.tensor_tensor(one_hot[:, k, :, :], tmp[:, 0, :, :], bc(top[:, free, :]), ALU.is_equal))
                yield

            def take(it, name, i):
                b = it.b
                dve.wait_ge(fill_ready, it.made(name, i))
                if name in ("x_turn", "attn_turn", "row_turn"):
                    to = {"x_turn": x_t, "attn_turn": attn_t, "row_turn": row_t}[name]
                    dve.tensor_copy(to[:, i, :], spare[:, :]).then_inc(fill_taken, 1)
                elif name in ("q", "k"):
                    c = i if name == "q" else KC + i
                    n = N if name == "q" else KCOLS[i % KCHUNK + 1] - KCOLS[i % KCHUNK]
                    dve.wait_ge(high_ready, (b + 1) * CHUNKS + c + 1)
                    dve.scalar_tensor_tensor(out=resid[:, c % 2, 0:n], in0=spare[:, 0:n],
                                             scalar=D ** -0.5 if name == "q" else 1.0, in1=parts[:, c % 2, 0, 0:n],
                                             op0=ALU.mult, op1=ALU.subtract).then_inc(fill_taken, 1)
                elif name == "o_turn":
                    of = spare[:, :].rearrange("p (t j c) -> p t j c", t=NT, j=GH)
                    dve.reciprocal(rden[:, :, :], of[:, :, :, DH]).then_inc(rden_ready, 1)
                    dve.wait_ge(rden_ready, b * G + i + 1 if i < G - 1 else b * G)
                    dve.tensor_tensor(attn[:, :, i * GH * DH:(i + 1) * GH * DH].rearrange("p t (j c) -> p t j c", j=GH),
                                      of[:, :, :, 0:DH], rden[:, :, :].unsqueeze(3).to_broadcast([P, NT, GH, DH]),
                                      ALU.mult).then_inc(fill_taken, 1)
                elif name == "out_proj":
                    if i == 0:
                        dve.wait_ge(x2_loaded, b * 16)
                    view = x2[:, 2 * i:2 * i + 2, :].rearrange("p t c -> p (t c)")
                    dve.scalar_tensor_tensor(out=view, in0=spare[:, :], scalar=tgx[:, 0:1], in1=view,
                                             op0=ALU.mult, op1=ALU.add).then_inc(fill_taken, 1)
                elif name == "logits":
                    lg = spare[:, 0:NT * E].rearrange("p (t e) -> p t e", t=NT)
                    dve.tensor_reduce(top[:, 7, :], lg, AX.X, ALU.max).then_inc(logits_max, 1)
                    dve.wait_ge(logits_max, b)
                    dve.tensor_tensor(prob[:, 0, :, :], lg, bc(top[:, 7, :]), ALU.subtract).then_inc(fill_taken, 1)
                elif name == "prefix":
                    dve.tensor_tensor(slot[:, :, :], spare[:, 0:NT * E].rearrange("p (t e) -> p t e", t=NT),
                                      region_at[:, :].unsqueeze(1).to_broadcast([P, NT, E]), ALU.add).then_inc(fill_taken, 1)

            def route(b, chain):
                dve.wait_ge(route_exp, b)
                chain(dve.tensor_reduce(top[:, 6, :], prob[:, 1, :, :], AX.X, ALU.add))
                yield
                chain(dve.reciprocal(top[:, 7, :], top[:, 6, :]))
                yield
                chain(dve.tensor_tensor(prob[:, 0, :, :], prob[:, 1, :, :], bc(top[:, 7, :]), ALU.mult))
                yield
                yield from pick(chain, 0, prob[:, 0, :, :], 2)
                chain(dve.tensor_scalar(tmp[:, 0, :, :], one_hot[:, 0, :, :], -2.0, None, ALU.mult))
                yield
                chain(dve.tensor_tensor(prob[:, 2, :, :], prob[:, 0, :, :], tmp[:, 0, :, :], ALU.add))
                yield
                yield from pick(chain, 1, prob[:, 2, :, :], 3)
                chain(dve.tensor_tensor(top[:, 6, :], top[:, 0, :], top[:, 1, :], ALU.add))
                yield
                chain(dve.reciprocal(top[:, 7, :], top[:, 6, :]))
                yield
                chain(dve.tensor_scalar(top[:, 7, :], top[:, 7, :], tgf[:, 0:1], None, ALU.mult))
                yield
                chain(dve.tensor_tensor(top[:, 4:6, :], top[:, 0:2, :],
                                        top[:, 7, :].unsqueeze(1).to_broadcast([P, 2, NT]), ALU.mult))
                yield
                chain(dve.tensor_tensor(chosen[:, :, :], one_hot[:, 0, :, :], one_hot[:, 1, :, :], ALU.add))
                yield
                chain(dve.tensor_copy(seen_at[:, 0, :], seen[:, :]))
                yield
                for t in range(1, NT):
                    chain(dve.tensor_tensor(seen_at[:, t, :], seen_at[:, t - 1, :], chosen[:, t - 1, :], ALU.add))
                    yield
                chain(dve.tensor_tensor(seen[:, :], seen_at[:, NT - 1, :], chosen[:, NT - 1, :], ALU.add))
                yield

            def place_rows(it, chain):
                dve.wait_ge(fill_taken, it.made("prefix", 0))
                chain(dve.tensor_tensor(tmp[:, :, :, :], slot[:, :, :].unsqueeze(1).to_broadcast([P, 2, NT, E]),
                                        one_hot[:, :, :, :], ALU.mult))
                yield
                chain(dve.tensor_reduce(top[:, 6:8, :], tmp[:, :, :, :], AX.X, ALU.add))
                yield
                chain(dve.tensor_copy(place[:, :, :], top[:, 6:8, :]))
                yield
                chain(dve.tensor_copy(routed_rows[:, :, :, D], top[:, 4:6, :]))
                yield
                chain(dve.tensor_copy(routed_rows[:, :, :, D + 1].bitcast(U32),
                                      token[:, :].unsqueeze(1).to_broadcast([P, 2, NT])))
                yield
                chain(dve.tensor_scalar(token[:, :], token[:, :], float(N), None, ALU.add))
                yield

            def reciprocals(b, s):
                r = rows_of(s % LT)
                dve.wait_ge(exp_done, b * UNITS + 2 * s + 2)
                dve.reciprocal(rz[0:r, s % RING, :], z[0:r, s % RING, :]).then_inc(rz_ready, 1)

            def take_acc(b, g):
                dve.wait_ge(pv_done, b * STEPS + (g + 1) * LT)
                dve.tensor_copy(o_acc[:, :], acc[:, :]).then_inc(acc_taken, 1)

            def run(it):
                b = it.b
                for s in range(STEPS):
                    for p in range(2):
                        if it.cur:
                            u = 2 * s + p
                            r = rows_of(s % LT)
                            dve.wait_ge(scores_ready, b * UNITS + u + 1)
                            dve.tensor_reduce(negmax[0:r, u % 4, :], scores[0:r, 2 * (u % SLOTS):2 * (u % SLOTS) + 2, :],
                                              AX.X, ALU.max, negate=True).then_inc(negmax_ready, 1)
                        if p == 0 and s == 2 and it.tail:
                            take_acc(b - 1, G - 1)
                        if p == 0 and it.cur and s in (LT + 2, 2 * LT + 2, 3 * LT + 2):
                            take_acc(b, s // LT - 1)
                        if p == 1 and s == 0 and it.tail:
                            reciprocals(b - 1, STEPS - 1)
                        if p == 1 and s > 0 and it.cur:
                            reciprocals(b, s - 1)
                        f = it.fill(s)
                        if f and f[0] != "v" and p == (f[0] in ("q", "k")):
                            take(it, *f)
                        if p == 1 and it.tail and s == 7:
                            dve.wait_ge(fill_taken, it.made("out_proj", 1))
                        if p == 1 and it.tail and s in (8, 9):
                            for t in range(2 * (s - 8), 2 * (s - 8) + 2):
                                dve.bn_stats(stats2[:, t, :], x2[:, t, :]).then_inc(stats2_done, 1)
                        if p == 1 and it.tail and s == 10:
                            wait_apart(dve, stats2_done, b * NT, passed_dve)
                            for t in range(NT):
                                dve.bn_aggr(mv2[:, t, :], stats2[:, t, :]).then_inc(mv2_ready, 1)
                        if p == 0 and it.next and 10 <= s < 10 + NT:
                            t = s - 10
                            if t == 0:
                                dve.wait_ge(x_loaded, (b + 2) * 16)
                            dve.bn_stats(stats1[:, t, :], x_in[:, t, :]).then_inc(stats_done, 1)
                        if p == 1 and it.next and s == 14:
                            wait_apart(dve, stats_done, (b + 2) * NT, passed_dve)
                            for t in range(NT):
                                dve.bn_aggr(mv1[:, t, :], stats1[:, t, :]).then_inc(mv_ready, 1)
                        if it.tail and s == 22 and p == 0:
                            routing = Chain(dve, route_step, (b - 1) * ROUTE_STEPS)
                            route_steps = route(b, routing)
                        if it.tail and 22 <= s < 22 + (ROUTE_STEPS + 1) // 2:
                            in_turn(routing, route_steps)
                        if it.tail and s == 38 and p == 0:
                            routing.settle()
                            placing = Chain(dve, place_step, (b - 1) * PLACE_STEPS)
                            place_steps = place_rows(it, placing)
                        if it.tail and 38 <= s < 38 + PLACE_STEPS // 2:
                            in_turn(placing, place_steps)

            over_batches(dve, run)

        @block.gpsimd
        def _(pool):
            pool.memset(ident[:, :], 0.0).then_inc(keep["built"], 1)
            pool.memset(tri[:, :], 1.0).then_inc(keep["built"], 1)
            pool.memset(ones[:, :], 1.0).then_inc(keep["built"], 1)
            pool.memset(pad_row[:, 0:D + 1], 0.0).then_inc(keep["built"], 1)
            pool.iota(token[:, :], pattern=[[P, NT]], base=0, channel_multiplier=1,
                      allow_small_or_imprecise_dtypes=True).then_inc(keep["built"], 1)
            pool.iota(pad_row[:, D + 1:D + 2].bitcast(U32), pattern=[[0, 1]], base=TOKENS,
                      channel_multiplier=1).then_inc(keep["built"], 1)
            pool.wait_ge(keep["built"], 6)
            pool.affine_select(out=ident[:, :], in_=ident[:, :], compare_op=ALU.not_equal, fill=1.0, base=0,
                               pattern=[[-1, P]], channel_multiplier=1).then_inc(keep["built"], 1)
            pool.affine_select(out=tri[:, :], in_=tri[:, :], compare_op=ALU.is_gt, fill=0.0, base=0,
                               pattern=[[1, P]], channel_multiplier=-1).then_inc(keep["built"], 1)
            pool.wait_ge(keep["built"], 8)
            pool.drain().then_inc(constants, 1)
            pool.dma_start(out[TOKENS:TOKENS + P, :], pad_row[:, 0:D]).then_inc(rows_out, 16)
            pool.wait_ge(dve_setup, DVE_SETUP)

            def one_over_deviation(mv, rstd, step, before):
                pool.tensor_scalar(rstd[:, 0, :], mv[:, :, 1], EPS, None, ALU.add).then_inc(step, 1)
                pool.wait_ge(step, before + 1)
                pool.tensor_tensor(rstd[:, 1, :], rstd[:, 0, :], minus_half[:, :], ALU.pow).then_inc(step, 1)
                pool.wait_ge(step, before + 2)

            def by_row(op, out, in0, factor, half):
                t = slice(2 * half, 2 * half + 2)
                return pool.tensor_tensor(out[:, t, 0:D], in0[:, t, 0:D], factor[:, t].unsqueeze(2).to_broadcast([P, 2, D]), op)

            def weigh_values(b, s):
                g, lt = s // LT, s % LT
                r = rows_of(lt)
                pool.wait_ge(rz_ready, b * STEPS + s + 1)
                wait(pool, pv_done, b * STEPS + s - RING + 1)
                pool.tensor_tensor(vz[0:r, s % RING, :, 0:DH + 1], v_ones[0:r, b % 2, lt, g * GH:(g + 1) * GH, :],
                                   rz[0:r, s % RING, :].unsqueeze(2).to_broadcast([r, GH, DH + 1]),
                                   ALU.mult).then_inc(vz_ready, 1)

            def run(it):
                b = it.b
                for s in range(STEPS):
                    if s == 0 and it.cur:
                        pool.wait_ge(fill_taken, it.base)
                    if it.cur and s >= 1:
                        weigh_values(b, s - 1)
                    if it.tail and s == 0:
                        weigh_values(b - 1, STEPS - 1)
                    if it.tail and s == 11:
                        wait_apart(pool, mv2_ready, b * NT, passed_pool)
                        one_over_deviation(mv2, rstd2, rstd2_step, (b - 1) * 2)
                        pool.wait_ge(rows_out, (b - 1) * 2 * NT * 16 + 16)
                    if it.tail and s in (11, 12):
                        by_row(ALU.subtract, routed_rows[:, 1, :, :], x2, mv2[:, :, 0], s - 11).then_inc(centred2, 1)
                    if it.tail and s in (12, 13):
                        pool.wait_ge(centred2, 2 * b)
                        by_row(ALU.mult, routed_rows[:, 0, :, :], routed_rows[:, 1, :, :], rstd2[:, 1, :], s - 12).then_inc(rows_ready, 1)
                    if it.tail and s in (14, 15):
                        pool.wait_ge(rows_ready, 2 * b)
                        by_row(ALU.mult, routed_rows[:, 1, :, :], routed_rows[:, 1, :, :], rstd2[:, 1, :], s - 14).then_inc(rows1_ready, 1)
                    if it.next and s == 15:
                        wait_apart(pool, mv_ready, (b + 2) * NT, passed_pool)
                        one_over_deviation(mv1, rstd1, rstd_step, (b + 1) * 2)
                    if it.next and s in (16, 17):
                        by_row(ALU.subtract, x_in, x_in, mv1[:, :, 0], s - 16).then_inc(centred1, 1)
                    if it.next and s in (18, 19):
                        pool.wait_ge(centred1, 2 * (b + 2))
                        by_row(ALU.mult, x_in, x_in, rstd1[:, 1, :], s - 18).then_inc(xn_ready, 1)
                    f = it.fill(s - 1) if s else None
                    if f and f[0] in ("q", "k"):
                        name, i = f
                        c = i if name == "q" else KC + i
                        n = N if name == "q" else KCOLS[i % KCHUNK + 1] - KCOLS[i % KCHUNK]
                        pool.wait_ge(middle_ready, (b + 1) * CHUNKS + c + 1)
                        pool.tensor_tensor(parts[:, c % 2, 2, 0:n], resid[:, c % 2, 0:n], parts[:, c % 2, 1, 0:n],
                                           ALU.subtract).then_inc(parts_ready, 1)
                    f = it.fill(s)
                    if f and f[0] in ("q", "k"):
                        name, i = f
                        c = i if name == "q" else KC + i
                        n = N if name == "q" else KCOLS[i % KCHUNK + 1] - KCOLS[i % KCHUNK]
                        pool.wait_ge(fill_taken, it.made(name, i))
                        pool.tensor_tensor(parts[:, c % 2, 1, 0:n], resid[:, c % 2, 0:n], zero[:, 0:1].to_broadcast([P, n]),
                                           ALU.add).then_inc(middle_ready, 1)
                    if it.tail and STEPS - 2 * NT <= s:
                        k, t = (s - STEPS + 2 * NT) // NT, (s - STEPS + 2 * NT) % NT
                        if s == STEPS - 2 * NT:
                            pool.wait_ge(rows1_ready, 2 * b)
                            wait_apart(pool, place_step, b * PLACE_STEPS, passed_pool)
                        pool.indirect_dma_start(
                            out=routed, out_offset=bass.IndirectOffsetOnAxis(place[:, k, t:t + 1], 0),
                            in_=routed_rows[:, k, t, :], in_offset=None).then_inc(rows_out, 16)

            over_batches(pool, run)
            pool.wait_ge(rows_out, B * 2 * NT * 16 + 16)


def experts(nc, keep, w1, w2, routed, out):
    ident, ones, seen, pad_row = keep["ident"], keep["ones"], keep["seen"], keep["pad_row"]
    HC = HID // P
    HB = BLK // P
    w1_rows = w1.rearrange("e (k p) h -> e p k h", p=P)
    w2_rows = w2.rearrange("e (k p) c -> e p k c", p=P)
    MIDDLE = NBLK - 5
    assert MIDDLE % 2 == 0

    with ExitStack() as ctx:
        def sb(name, shape, dt=F32):
            return ctx.enter_context(nc.sbuf_tensor(name, shape, dt))

        def psum(name, shape):
            return ctx.enter_context(nc.psum_tensor(name, shape, F32))

        def sem(name):
            return ctx.enter_context(nc.semaphore(name))

        rows = sb("rows", [P, 2, HB, ROW])
        w1_sb = sb("w1_sb", [P, 2, KC, HID])
        w2_sb = sb("w2_sb", [P, 2, HC, D])
        rows_t = sb("rows_t", [P, 2, KC, BLK])
        hidden = sb("hidden", [P, 2, HC, BLK])
        gate_token = sb("gate_token", [P, 2, HB, 2])
        result = sb("result", [P, 2, HB, D])
        count = sb("count", [P, E])
        count_up = sb("count_up", [P, E], I32)
        blocks_i = sb("blocks_i", [P, E], I32)
        blocks_of = sb("blocks_of", [P, E])
        ones_e = sb("ones_e", [P, E])
        last_of = sb("last_of", [P, E])
        region_of = sb("region_of", [P, E])
        pad_at = sb("pad_at", [P, E])
        number = sb("number", [P, NBLK])
        past = sb("past", [P, NBLK, E])
        expert_f = sb("expert_f", [P, NBLK])
        first_f = sb("first_f", [P, NBLK])
        row_f = sb("row_f", [P, NBLK])
        plan = sb("plan", [P, 3, NBLK], I32)

        ps_count = psum("ps_count", [P, 512])
        ps_rows = psum("ps_rows", [P, 512])
        ps_hidden = psum("ps_hidden", [P, 4, 512])
        ps_y = psum("ps_y", [P, 2, 512])

        numbers = sem("numbers")
        counted = sem("counted")
        plan_step = sem("plan_step")
        plan_ready = sem("plan_ready")
        pads_in = sem("pads_in")
        rows_in = [sem(f"rows_in_{slot}") for slot in range(2)]
        w1_in = [sem(f"w1_in_{slot}") for slot in range(2)]
        w2_in = [sem(f"w2_in_{slot}") for slot in range(2)]
        turned = sem("turned")
        rows_taken = sem("rows_taken")
        gates_taken = sem("gates_taken")
        hidden_ready = sem("hidden_ready")
        gelu_done = sem("gelu_done")
        y_ready = sem("y_ready")
        scaled = sem("scaled")
        added = sem("added")
        passed_sp, passed_pool = (sem(f"passed_in_experts_{e}") for e in ("sp", "pool"))

        block = ctx.enter_context(nc.Block())

        def over_blocks(eng, run):
            run(1, 1, False)
            run(2, 0, False)
            with eng.Fori(0, MIDDLE // 2) as i:
                run(i * 2 + 3, 1, False)
                run(i * 2 + 4, 0, False)
            run(NBLK - 2, (NBLK - 2) % 2, False)
            run(NBLK - 1, (NBLK - 1) % 2, True)

        @block.sync
        def _(sp):
            sp.wait_ge(plan_ready, 1)
            with sp.Fori(0, E) as e:
                at = nc.values_load(plan[0:1, 2, bass.ds(e, 1)], engines=[SP_ENGINE], min_val=0, max_val=SPARE)
                for half in range(HB):
                    sp.dma_start(routed[bass.ds(at + half * P, P), :], pad_row[:, :]).then_inc(pads_in, 16)
            for half in range(HB):
                sp.dma_start(routed[SPARE + half * P:SPARE + (half + 1) * P, :], pad_row[:, :]).then_inc(pads_in, 16)
            sp.wait_ge(pads_in, (E + 1) * HB * 16)

            def load(j, slot):
                e = nc.values_load(plan[0:1, 0, bass.ds(j, 1)], engines=[SP_ENGINE], min_val=0, max_val=E - 1)
                at = nc.values_load(plan[0:1, 1, bass.ds(j, 1)], engines=[SP_ENGINE], min_val=0, max_val=SPARE)
                wait(sp, rows_taken, j - 1)
                wait(sp, gates_taken, j - 1)
                sp.dma_start(rows[:, slot, :, :], routed[bass.ds(at, BLK), :].rearrange("(h p) c -> p h c", p=P)).then_inc(rows_in[slot], 16)
                if not isinstance(j, int) or j > 1:
                    wait_apart(sp, hidden_ready, (j - 1) * (HC // 2), passed_sp)
                sp.dma_start(w1_sb[:, slot, :, :], w1_rows[e]).then_inc(w1_in[slot], 16)
                if not isinstance(j, int) or j > 1:
                    wait_apart(sp, y_ready, (j - 1) * HB, passed_sp)
                sp.dma_start(w2_sb[:, slot, :, :], w2_rows[e]).then_inc(w2_in[slot], 16)

            load(0, 0)
            load(1, 1)
            with sp.Fori(0, (NBLK - 3) // 2) as i:
                load(i * 2 + 2, 0)
                load(i * 2 + 3, 1)
            load(NBLK - 1, (NBLK - 1) % 2)

        @block.tensor
        def _(pe):
            pe.wait_ge(numbers, 1)
            pe.matmul(ps_count[:, 0:E], ones[:, :], seen[:, :], start=True, stop=True).then_inc(counted, 1)

            def turn(j, slot):
                pe.wait_ge(rows_in[slot], (j // 2 + 1) * 16)
                wait(pe, rows_taken, j)
                for k in range(KC):
                    for half in range(HB):
                        mm = pe.transpose(ps_rows[:, (k * HB + half) * P:(k * HB + half + 1) * P],
                                          rows[:, slot, half, k * P:(k + 1) * P], ident[:, :])
                mm.then_inc(turned, 1)

            def first(j, slot):
                pe.wait_ge(rows_taken, j + 1)
                pe.wait_ge(w1_in[slot], (j // 2 + 1) * 16)
                for h in range(HC):
                    if h % 2 == 0:
                        wait(pe, gelu_done, (j - 1) * (HC // 2) + h // 2 + 1)
                    for k in range(KC):
                        mm = pe.matmul(ps_hidden[:, h // 2, (h % 2) * BLK:(h % 2 + 1) * BLK],
                                       w1_sb[:, slot, k, h * P:(h + 1) * P], rows_t[:, slot, k, :],
                                       start=(k == 0), stop=(k == KC - 1))
                    if h % 2:
                        mm.then_inc(hidden_ready, 1)

            def second(j, slot, half):
                if half == 0:
                    pe.wait_ge(w2_in[slot], (j // 2 + 1) * 16)
                    pe.wait_ge(gelu_done, (j + 1) * (HC // 2))
                    wait(pe, scaled, (j - 1) * HB)
                for h in range(HC):
                    mm = pe.matmul(ps_y[:, slot, half * D:(half + 1) * D], hidden[:, slot, h, half * P:(half + 1) * P],
                                   w2_sb[:, slot, h, :], start=(h == 0), stop=(h == HC - 1))
                mm.then_inc(y_ready, 1)

            def run(j, slot, last):
                first(j, slot)
                second(j - 1, 1 - slot, 0)
                if not last:
                    turn(j + 1, 1 - slot)
                second(j - 1, 1 - slot, 1)

            turn(0, 0)
            first(0, 0)
            turn(1, 1)
            over_blocks(pe, run)
            for half in range(HB):
                second(NBLK - 1, (NBLK - 1) % 2, half)

        @block.scalar
        def _(act):
            def run(j, slot, last):
                for q in range(HC // 2):
                    act.wait_ge(hidden_ready, j * (HC // 2) + q + 1)
                    if q == 0:
                        wait(act, y_ready, (j - 1) * HB)
                    act.activation(hidden[:, slot, 2 * q:2 * q + 2, :].rearrange("p h n -> p (h n)"), ps_hidden[:, q, :],
                                   ACT.Gelu).then_inc(gelu_done, 1)

            run(0, 0, False)
            over_blocks(act, run)

        @block.vector
        def _(dve):
            steps = Chain(dve, plan_step, 0)

            def chain(ins):
                steps(ins)
                steps.settle()

            chain(dve.memset(ones_e[:, :], 1.0))
            for e in range(E):
                chain(dve.memset(region_of[:, e:e + 1], float(e * REGION)))
            dve.wait_ge(numbers, 1)
            dve.wait_ge(counted, 1)
            chain(dve.tensor_copy(count[:, :], ps_count[:, 0:E]))
            chain(dve.tensor_scalar(count_up[:, :], count[:, :], float(BLK - 1), None, ALU.add))
            chain(dve.tensor_scalar(blocks_i[:, :], count_up[:, :], BLK.bit_length() - 1, None, ALU.logical_shift_right))
            chain(dve.tensor_copy(blocks_of[:, :], blocks_i[:, :]))
            chain(dve.tensor_tensor_scan(last_of[:, :], ones_e[:, :], blocks_of[:, :], 0.0, ALU.mult, ALU.add))
            chain(dve.tensor_tensor(past[:, :, :], number[:, :].unsqueeze(2).to_broadcast([P, NBLK, E]),
                                    last_of[:, :].unsqueeze(1).to_broadcast([P, NBLK, E]), ALU.is_ge))
            chain(dve.tensor_reduce(expert_f[:, :], past[:, :, :], AX.X, ALU.add))
            chain(dve.tensor_tensor(past[:, :, :], past[:, :, :],
                                    blocks_of[:, :].unsqueeze(1).to_broadcast([P, NBLK, E]), ALU.mult))
            chain(dve.tensor_reduce(first_f[:, :], past[:, :, :], AX.X, ALU.add))
            chain(dve.tensor_tensor(row_f[:, :], number[:, :], first_f[:, :], ALU.subtract))
            chain(dve.tensor_scalar(row_f[:, :], row_f[:, :], float(BLK), None, ALU.mult))
            chain(dve.tensor_scalar(first_f[:, :], expert_f[:, :], float(REGION), None, ALU.mult))
            chain(dve.tensor_tensor(row_f[:, :], row_f[:, :], first_f[:, :], ALU.add))
            chain(dve.tensor_scalar(row_f[:, :], row_f[:, :], float(SPARE), None, ALU.min))
            chain(dve.tensor_scalar(expert_f[:, :], expert_f[:, :], float(E - 1), None, ALU.min))
            chain(dve.tensor_tensor(pad_at[:, :], count[:, :], region_of[:, :], ALU.add))
            chain(dve.tensor_copy(plan[:, 0, :], expert_f[:, :]))
            chain(dve.tensor_copy(plan[:, 1, :], row_f[:, :]))
            dve.tensor_copy(plan[:, 2, 0:E], pad_at[:, :]).then_inc(plan_ready, 1)

            def take_rows(j, slot):
                dve.wait_ge(turned, j + 1)
                dve.tensor_copy(rows_t[:, slot, :, :].rearrange("p k n -> p (k n)"), ps_rows[:, :]).then_inc(rows_taken, 1)

            def take_gates(j, slot):
                wait(dve, added, (j - 1) * HB * 16)
                dve.wait_ge(rows_in[slot], (j // 2 + 1) * 16)
                dve.tensor_copy(gate_token[:, slot, :, :], rows[:, slot, :, D:ROW]).then_inc(gates_taken, 1)

            def scale(j, slot, half):
                dve.wait_ge(y_ready, (j + 1) * HB)
                dve.tensor_scalar(result[:, slot, half, :], ps_y[:, slot, half * D:(half + 1) * D],
                                  gate_token[:, slot, half, 0:1], None, ALU.mult).then_inc(scaled, 1)

            def run(j, slot, last):
                if not last:
                    take_rows(j + 1, 1 - slot)
                for half in range(HB):
                    if half == 0:
                        dve.wait_ge(gates_taken, j)
                        wait(dve, added, (j - 2) * HB * 16)
                    scale(j - 1, 1 - slot, half)
                if not last:
                    take_gates(j + 1, 1 - slot)

            take_rows(0, 0)
            take_gates(0, 0)
            take_rows(1, 1)
            take_gates(1, 1)
            over_blocks(dve, run)
            for half in range(HB):
                if half == 0:
                    dve.wait_ge(gates_taken, NBLK)
                    wait(dve, added, (NBLK - 2) * HB * 16)
                scale(NBLK - 1, (NBLK - 1) % 2, half)

        @block.gpsimd
        def _(pool):
            pool.iota(number[:, :], pattern=[[1, NBLK]], base=0, channel_multiplier=0,
                      allow_small_or_imprecise_dtypes=True).then_inc(numbers, 1)

            def add(j, slot):
                for half in range(HB):
                    pool.wait_ge(scaled, j * HB + half + 1)
                    if not (isinstance(j, int) and j == 0 and half == 0):
                        wait_apart(pool, added, (j * HB + half) * 16, passed_pool)
                    pool.indirect_dma_start(
                        out=out, out_offset=bass.IndirectOffsetOnAxis(gate_token[:, slot, half, 1:2].bitcast(U32), 0),
                        in_=result[:, slot, half, :], in_offset=None, compute_op=ALU.add).then_inc(added, 16)

            add(0, 0)
            over_blocks(pool, lambda j, slot, last: add(j, slot))
            pool.wait_ge(added, NBLK * HB * 16)


def flamingo_block(nc, x, ctx_t, g_xattn, g_ffn, wq_t, wk_t, wv_t, wo_t, router_t, w1, w2, out):
    routed = nc.dram_tensor("routed", (SPARE + BLK, ROW), F32, kind="Internal").ap()
    q_parts_dram = nc.dram_tensor("q_parts", (3, D, N), BF16, kind="Internal").ap()
    k_parts_dram = nc.dram_tensor("k_parts", (3, D, L), BF16, kind="Internal").ap()
    with ExitStack() as ctx:
        keep = {name: ctx.enter_context(nc.sbuf_tensor(name, [P, n], F32))
                for name, n in (("ident", P), ("tri", P), ("ones", P), ("seen", E), ("pad_row", ROW))}
        keep["built"] = ctx.enter_context(nc.semaphore("built"))
        attention_and_routing(nc, keep, x, ctx_t, g_xattn, g_ffn, wq_t, wk_t, wv_t, wo_t, router_t,
                              out, routed, q_parts_dram, k_parts_dram)
        experts(nc, keep, w1, w2, routed, out)


def kernel(**inputs):
    import numpy as np
    import concourse.bacc as bacc
    from concourse.bass_utils import run_bass_kernel_spmd

    def turned(a):
        return np.ascontiguousarray(np.swapaxes(np.asarray(a), -1, -2))

    nc = bacc.Bacc("TRN2", target_bir_lowering=False, num_devices=1)
    given = [
        ("x", np.ascontiguousarray(inputs["x"])),
        ("ctx_t", turned(inputs["ctx_1024"])),
        ("g_xattn", np.ascontiguousarray(inputs["g_xattn"])),
        ("g_ffn", np.ascontiguousarray(inputs["g_ffn"])),
        ("wq_t", turned(inputs["L0_xattn_Wq"])),
        ("wk_t", turned(inputs["L0_xattn_Wk"])),
        ("wv_t", turned(inputs["L0_xattn_Wv"])),
        ("wo_t", turned(inputs["L0_xattn_Wo"])),
        ("router_t", turned(inputs["L0_ffn_router_w"])),
        ("w1", np.ascontiguousarray(inputs["L0_ffn_w1"])),
        ("w2", np.ascontiguousarray(inputs["L0_ffn_w2"])),
    ]
    arrays = {f"in_{name}": a for name, a in given}
    args = [nc.dram_tensor(f"in_{name}", a.shape, mybir.dt.from_np(a.dtype), kind="ExternalInput").ap()
            for name, a in given]
    out = nc.dram_tensor("out", (TOKENS + P, D), F32, kind="ExternalOutput").ap()
    flamingo_block(nc, *args, out)
    r = run_bass_kernel_spmd(nc, [arrays], core_ids=[0])
    return r.results[0]["out"][0:TOKENS].reshape(B, N, D)
```

```python
from contextlib import ExitStack

import numpy as np

import concourse.bass as bass
from concourse import mybir

ALU = mybir.AluOpType
ACT = mybir.ActivationFunctionType
AX = mybir.AxisListType
F32 = mybir.dt.float32
BF16 = mybir.dt.bfloat16
I32 = mybir.dt.int32
U32 = mybir.dt.uint32
SP_ENGINE = mybir.EngineType.SP
DVE_ENGINE = mybir.EngineType.DVE

P = 128
B, N, D = 8, 512, 256
L = 1601
H = 16
DH = D // H
E, HID = 8, 1024
EPS = 1e-5
KC = D // P
NT = N // P
LT = (L + P - 1) // P
GH = 4
G = H // GH
STEPS = G * LT
UNITS = 2 * STEPS
RING = 4
SLOTS = 3
K_PART = (0, 0, 0, 1, 1, 1, 2, 2)
Q_PART = (0, 1, 2, 0, 1, 2, 0, 1)
BLOCKS = len(K_PART)
KCHUNK = 4
KCOLS = [(L * i) // KCHUNK for i in range(KCHUNK + 1)]
KCMAX = max(KCOLS[i + 1] - KCOLS[i] for i in range(KCHUNK))
CHUNKS = KC + KC * KCHUNK
VF = (LT + 1) // 2
TOKENS = B * N
ROW = D + 2
BLK = 128
REGION = TOKENS + BLK
SPARE = E * REGION
NBLK = (2 * TOKENS) // BLK + E - 1
HC = HID // P
LOADS = 16 * 2 * BLOCKS

FILL_AT = {
    3: ("tail", "o_turn", 3), 5: ("tail", "attn_turn", 1), 6: ("tail", "out_proj", 0),
    8: ("tail", "out_proj", 1), 10: ("next", "v", 0), 12: ("next", "v", 1), 14: ("next", "v", 2),
    16: ("cur", "o_turn", 0), 17: ("tail", "row_turn", 0), 18: ("tail", "row_turn", 1),
    20: ("tail", "logits", 0), 21: ("next", "x_turn", 0), 22: ("next", "x_turn", 1), 23: ("next", "q", 0),
    25: ("next", "q", 1), 27: ("next", "k", 0), 29: ("next", "k", 1), 30: ("cur", "o_turn", 1),
    31: ("next", "k", 2), 33: ("next", "k", 3), 35: ("next", "k", 4), 36: ("tail", "prefix", 0),
    37: ("next", "k", 5), 39: ("next", "k", 6), 41: ("next", "k", 7), 42: ("cur", "o_turn", 2),
    43: ("cur", "attn_turn", 0), 45: ("next", "v", 3), 47: ("next", "v", 4), 49: ("next", "v", 5),
    51: ("next", "v", 6),
}
FIRST_FILL_AT = {s + 21: ("next", name, i) for s, (name, i) in enumerate(
    [("k", i) for i in range(KCHUNK)] + [("x_turn", 0), ("x_turn", 1), ("q", 0)] +
    [("k", i) for i in range(KCHUNK, 2 * KCHUNK)] + [("q", 1)] + [("v", i) for i in range(VF)])}
FIRST_ORDER = [KC + i for i in range(KCHUNK)] + [0] + [KC + i for i in range(KCHUNK, 2 * KCHUNK)] + [1]
EARLY = KCHUNK + 1
LOGITS = 20
ROUTE = 23
PLACE = 37
OUT = 8
STATS_X = (7, 11, 12, 13)
CENTRE_X = 16


class Iteration:

    def __init__(self, b, tail=True, cur=True, nxt=True):
        self.b, self.tail, self.cur, self.next = b, tail, cur, nxt
        has = {"tail": tail, "cur": cur, "next": nxt}
        self.first = isinstance(b, int) and b < 0
        self.table = FIRST_FILL_AT if self.first else FILL_AT
        order = [self.table[s] for s in sorted(self.table) if has[self.table[s][0]]]
        self.number = {(name, i): n for n, (_, name, i) in enumerate(order)}
        self.fills = len(order)
        full = len(FILL_AT)
        before = sum(1 for kind, _, _ in FILL_AT.values() if kind == "next")
        first = before + sum(1 for kind, _, _ in FILL_AT.values() if kind != "tail")
        if isinstance(b, int) and b < 1:
            self.base = (0, before)[b + 1]
        elif isinstance(b, int) and b == B:
            self.base = first + full * (B - 2) + full - before
        else:
            self.base = (b - 1) * full + first

    def fill(self, s):
        if s not in self.table:
            return None
        kind, name, i = self.table[s]
        return (name, i) if {"tail": self.tail, "cur": self.cur, "next": self.next}[kind] else None

    def two_banks(self, name, i):
        return self.first and name in ("k", "v") and i % KCHUNK > 0

    def chunk(self, name, i):
        c = i if name == "q" else KC + i
        n = N if name == "q" else KCOLS[i % KCHUNK + 1] - KCOLS[i % KCHUNK]
        return c, FIRST_ORDER.index(c) if self.first else c, n

    def made(self, name, i):
        return self.base + self.number[(name, i)] + 1


def over_batches(eng, run):
    run(Iteration(-1, tail=False, cur=False))
    run(Iteration(0, tail=False))
    with eng.Fori(1, B - 1) as b:
        run(Iteration(b))
    run(Iteration(B - 1, nxt=False))
    run(Iteration(B, cur=False, nxt=False))


def wait(eng, sem, value):
    if not (isinstance(value, int) and value <= 0):
        eng.wait_ge(sem, value)


def wait_apart(eng, sem, value, passed):
    eng.wait_ge(sem, value)
    eng.sem_inc(passed, 1)


class Chain:

    def __init__(self, eng, sem, before):
        self.eng, self.sem, self.n, self.any = eng, sem, before, False

    def __call__(self, ins):
        self.n, self.any = self.n + 1, True
        ins.then_inc(self.sem, 1)

    def settle(self):
        if self.any:
            self.eng.wait_ge(self.sem, self.n)


def in_turn(chain, steps):
    chain.settle()
    next(steps, None)


def rows_of(lt):
    return min(P, L - lt * P)


def attention_and_routing(nc, keep, x, ctx_t, g_xattn, g_ffn, wq_t, wk_t, wv_t, wo_t, router_t,
                          w1, w2, out, routed, q_parts_dram, k_parts_dram):
    ident, tri, ones, pad_row, plan = (keep[name] for name in ("ident", "tri", "ones", "pad_row", "plan"))
    w1_all, w2_all, pads_in, expert_in = (keep[name] for name in ("w1_all", "w2_all", "pads_in", "expert_in"))
    x_rows = x.rearrange("b (t p) c -> b p t c", p=P)
    out_rows = out[0:TOKENS, :].rearrange("(b t p) c -> b p t c", p=P, t=NT)
    ctx_rows = ctx_t.rearrange("b (k p) l -> b p k l", p=P)

    with ExitStack() as ctx:
        def sb(name, shape, dt=F32):
            return ctx.enter_context(nc.sbuf_tensor(name, shape, dt))

        def sem(name):
            return ctx.enter_context(nc.semaphore(name))

        def under(weights, at, shape, dt=F32):
            n = int(np.prod(shape)) * (2 if dt == BF16 else 4) // 4
            names = " ".join("abcdef"[0:len(shape)])
            flat = weights[:, at:at + n]
            return (flat.bitcast(dt) if dt != F32 else flat).rearrange(
                f"p ({names}) -> p {names}", **{"abcdef"[i]: n for i, n in enumerate(shape)})

        k_stack = under(w1_all, 0, [G, GH, L], BF16)
        ctx_sb = under(w1_all, G * GH * L // 2, [KC, L])
        probs = under(w2_all, 0, [RING, GH, N])
        v_ones = under(w2_all, RING * GH * N, [2, LT, H, DH + 1])
        q_stack = sb("q_stack", [P, G, GH, N], BF16)
        vz = sb("vz", [P, RING, GH, 32])
        x_in = sb("x_in", [P, NT, D])
        x_t = sb("x_t", [P, KC, N])
        x2 = sb("x2", [P, NT, D])
        routed_rows = sb("routed_rows", [P, 2, NT, ROW])
        parts = sb("parts", [P, 2, 3, N], BF16)
        resid = sb("resid", [P, 2, N])
        o_acc = sb("o_acc", [P, N])
        attn = sb("attn", [P, NT, D])
        attn_t = sb("attn_t", [P, KC, N])
        row_t = sb("row_t", [P, KC, N])
        wq_sb = sb("wq_sb", [P, KC, D])
        wk_sb = sb("wk_sb", [P, KC, D])
        wv_sb = sb("wv_sb", [P, KC, D])
        wo_sb = sb("wo_sb", [P, KC, D])
        router_sb = sb("router_sb", [P, KC, E])
        gx = sb("gx", [P, 1])
        gf = sb("gf", [P, 1])
        tgx = sb("tgx", [P, 1])
        tgf = sb("tgf", [P, 1])
        negmax = sb("negmax", [P, 4, 2])
        z = sb("z", [P, RING, GH])
        rz = sb("rz", [P, RING, GH])
        rden = sb("rden", [P, NT, GH])
        stats1 = sb("stats1", [P, NT, 6])
        mv1 = sb("mv1", [P, NT, 2])
        rstd1 = sb("rstd1", [P, 2, NT])
        stats2 = sb("stats2", [P, NT, 6])
        mv2 = sb("mv2", [P, NT, 2])
        rstd2 = sb("rstd2", [P, 2, NT])
        minus_half = sb("minus_half", [P, NT])
        prob = sb("prob", [P, 3, NT, E])
        one_hot = sb("one_hot", [P, 2, NT, E])
        tmp = sb("tmp", [P, 2, NT, E])
        zero = sb("zero", [P, 1])
        top = sb("top", [P, 8, NT])
        chosen = sb("chosen", [P, NT, E])
        seen_at = sb("seen_at", [P, NT, E])
        slot = sb("slot", [P, NT, E])
        region_at = sb("region_at", [P, E])
        first_of = sb("first_of", [P, E])
        token = sb("token", [P, NT])
        place = sb("place", [P, 2, NT], U32)
        seen = sb("seen", [P, E])
        count = sb("count", [P, E])
        count_up = sb("count_up", [P, E], I32)
        blocks_i = sb("blocks_i", [P, E], I32)
        blocks_of = sb("blocks_of", [P, E])
        ones_e = sb("ones_e", [P, E])
        last_of = sb("last_of", [P, E])
        pad_at = sb("pad_at", [P, E])
        number = sb("number", [P, NBLK])
        past = sb("past", [P, NBLK, E])
        expert_f = sb("expert_f", [P, NBLK])
        first_f = sb("first_f", [P, NBLK])
        row_f = sb("row_f", [P, NBLK])

        first_parts = under(w2_all, 0, [CHUNKS, 3, N], BF16)

        def parts_of(it, c):
            return first_parts[:, c] if it.first else parts[:, c % 2]

        def bank(it, name, i):
            return scores[:, 2 * SLOTS - 1, :] if it.first and name in ("k", "v") and i % 2 else spare

        scores = ctx.enter_context(nc.psum_tensor("scores", [P, 2 * SLOTS, N], F32))
        acc = ctx.enter_context(nc.psum_tensor("acc", [P, N], F32))
        spare = ctx.enter_context(nc.psum_tensor("spare", [P, N], F32))

        weights_in = sem("weights_in")
        wk_in = sem("wk_in")
        gates_in = sem("gates_in")
        constants = sem("constants")
        tanh_ready = sem("tanh_ready")
        dve_setup = sem("dve_setup")
        stack_in = [sem(f"stack_in_{g}") for g in range(G)]
        x_loaded = sem("x_loaded")
        ctx_loaded = sem("ctx_loaded")
        x2_loaded = sem("x2_loaded")
        scores_ready = sem("scores_ready")
        negmax_ready = sem("negmax_ready")
        exp_done = sem("exp_done")
        rz_ready = sem("rz_ready")
        vz_ready = sem("vz_ready")
        pv_done = sem("pv_done")
        acc_taken = sem("acc_taken")
        fill_ready = sem("fill_ready")
        fill_taken = sem("fill_taken")
        high_ready = sem("high_ready")
        middle_ready = sem("middle_ready")
        parts_ready = sem("parts_ready")
        parts_stored = [sem(f"parts_stored_{i}") for i in range(2)]
        stats_done = sem("stats_done")
        mv_ready = sem("mv_ready")
        rstd_step = sem("rstd_step")
        xn_ready = sem("xn_ready")
        rden_ready = sem("rden_ready")
        stats2_done = sem("stats2_done")
        mv2_ready = sem("mv2_ready")
        rstd2_step = sem("rstd2_step")
        rows_ready = sem("rows_ready")
        logits_max = sem("logits_max")
        route_exp = sem("route_exp")
        route_step = sem("route_step")
        place_step = sem("place_step")
        rows_out = sem("rows_out")
        x2_stored = sem("x2_stored")
        centred1 = sem("centred1")
        centred2 = sem("centred2")
        rows1_ready = sem("rows1_ready")
        counted = sem("counted")
        plan_step = sem("plan_step")
        pads_known = sem("pads_known")

        passed_sp, passed_dve, passed_pool = (sem(f"passed_{e}") for e in ("sp", "dve", "pool"))
        ROUTE_STEPS, PLACE_STEPS = 25, 6
        DVE_SETUP = 6 + 2 * E

        def load_w1(eng, e):
            eng.dma_start(w1_all[:, e * KC * HID:(e + 1) * KC * HID].rearrange("p (k h) -> p k h", k=KC),
                          w1[e].rearrange("(k p) h -> p k h", p=P)).then_inc(expert_in[e], 16)

        block = ctx.enter_context(nc.Block())

        EARLY_W1 = (G - 1) * (GH * L // 2) // (KC * HID)
        N_WEIGHTS = 4

        @block.sync
        def _(sp):
            for g_sb, g_in in ((gx, g_xattn), (gf, g_ffn)):
                sp.dma_start(g_sb[:, :], g_in.partition_broadcast(P)).then_inc(gates_in, 16)

            def run(it):
                b = it.b
                if it.next:
                    if it.cur:
                        wait_apart(sp, fill_taken, it.base, passed_sp)
                    sp.dma_start(x_in[:, :, :], x_rows[b + 1]).then_inc(x_loaded, 16)
                    if it.first:
                        sp.dma_start(wk_sb[:, :, :], wk_t.rearrange("(k p) n -> p k n", p=P)).then_inc(wk_in, 16)
                    sp.dma_start(ctx_sb[:, :, :], ctx_rows[b + 1]).then_inc(ctx_loaded, 16)
                    if it.first:
                        for w_sb, w in ((wq_sb, wq_t), (wv_sb, wv_t), (wo_sb, wo_t), (router_sb, router_t)):
                            sp.dma_start(w_sb[:, :, :], w.rearrange("(k p) n -> p k n", p=P)).then_inc(weights_in, 16)
                if it.cur:
                    wait(sp, scores_ready, b * UNITS)
                    load_stacks(3)
                if it.tail:
                    sp.dma_start(x2[:, :, :], x_rows[b - 1]).then_inc(x2_loaded, 16)
                    sp.wait_ge(fill_taken, it.made("out_proj", 1))
                    sp.dma_start(out_rows[b - 1], x2[:, :, :]).then_inc(x2_stored, 16)
                if it.next:
                    if it.cur:
                        for g in range(G):
                            sp.wait_ge(stack_in[g], (b + 1) * LOADS)
                    for at, c in enumerate(FIRST_ORDER if it.first else range(CHUNKS)):
                        sp.wait_ge(parts_ready, (b + 1) * CHUNKS + at + 1)
                        if c < KC:
                            sp.dma_start(q_parts_dram[:, c * P:(c + 1) * P, :].rearrange("s p n -> p s n"),
                                         parts_of(it, c)[:, :, :]).then_inc(parts_stored[c % 2], 16)
                        else:
                            m, i = (c - KC) // KCHUNK, (c - KC) % KCHUNK
                            n = KCOLS[i + 1] - KCOLS[i]
                            sp.dma_start(k_parts_dram[:, m * P:(m + 1) * P, KCOLS[i]:KCOLS[i + 1]].rearrange("s p n -> p s n"),
                                         parts_of(it, c)[:, :, 0:n]).then_inc(parts_stored[c % 2], 16)
                        if it.first and at == EARLY - 1:
                            for half in range(2):
                                sp.wait_ge(parts_stored[half], (EARLY + 1 - half) // 2 * 16)
                            load_stacks(0)
                    for half in range(2):
                        wait_apart(sp, parts_stored[half], (b + 2) * (CHUNKS // 2) * 16, passed_sp)
                    for g in range(1 if it.first else 0, G - 1):
                        if it.cur:
                            sp.wait_ge(scores_ready, b * UNITS + (g + 1) * 2 * LT)
                        load_stacks(g)
                if it.tail and not (isinstance(b, int) and b == B):
                    wait_apart(sp, x2_stored, b * 16, passed_sp)
                    wait_apart(sp, rows_ready, 2 * b, passed_sp)
                if isinstance(b, int) and b == B - 1:
                    for e in range(EARLY_W1):
                        groups = -(-(e + 1) * KC * HID // (GH * L // 2))
                        sp.wait_ge(scores_ready, b * UNITS + groups * 2 * LT)
                        load_w1(sp, e)

            def load_stacks(g):
                for blk in range(BLOCKS):
                    rows = slice(blk * DH, (blk + 1) * DH)
                    heads = slice(g * GH * DH, (g + 1) * GH * DH)
                    sp.dma_start(q_stack[rows, g, :, :], q_parts_dram[Q_PART[blk], heads, :].rearrange(
                        "(h c) n -> c h n", c=DH)).then_inc(stack_in[g], 16)
                    sp.dma_start(k_stack[rows, g, :, :], k_parts_dram[K_PART[blk], heads, :].rearrange(
                        "(h c) n -> c h n", c=DH)).then_inc(stack_in[g], 16)

            over_batches(sp, run)
            sp.dma_start(routed[SPARE:SPARE + BLK, :], pad_row[:, :]).then_inc(pads_in, 16)
            sp.wait_ge(pads_known, 1)
            for e in range(E):
                at = nc.values_load(plan[0:1, e + 2 * NBLK:e + 2 * NBLK + 1], engines=[SP_ENGINE], min_val=0, max_val=SPARE)
                sp.dma_start(routed[bass.ds(at, BLK), :], pad_row[:, :]).then_inc(pads_in, 16)
            sp.wait_ge(x2_stored, B * 16)

        @block.tensor
        def _(pe):
            pe.wait_ge(constants, 1)

            def fill(it, name, i):
                b = it.b
                spare = bank(it, name, i)
                if it.two_banks(name, i):
                    wait(pe, fill_taken, it.made(name, i) - 2)
                elif name != "logits":
                    wait(pe, fill_taken, it.made(name, i) - 1)
                if name == "x_turn":
                    pe.wait_ge(xn_ready, 2 * (b + 2))
                    for t in range(NT):
                        mm = pe.transpose(spare[:, t * P:(t + 1) * P], x_in[:, t, i * P:(i + 1) * P], ident[:, :])
                elif name == "q":
                    if it.first and i == 0:
                        pe.wait_ge(weights_in, N_WEIGHTS * 16)
                    for k in range(KC):
                        mm = pe.matmul(spare[:, :], wq_sb[:, k, i * P:(i + 1) * P], x_t[:, k, :],
                                       start=(k == 0), stop=(k == KC - 1))
                elif name == "k":
                    m, c = i // KCHUNK, i % KCHUNK
                    if it.first and i == 0:
                        pe.wait_ge(wk_in, 16)
                        pe.wait_ge(ctx_loaded, 16)
                    for k in range(KC):
                        mm = pe.matmul(spare[:, 0:KCOLS[c + 1] - KCOLS[c]], wk_sb[:, k, m * P:(m + 1) * P],
                                       ctx_sb[:, k, KCOLS[c]:KCOLS[c + 1]], start=(k == 0), stop=(k == KC - 1))
                elif name == "v":
                    if i == 0 and not it.first:
                        pe.wait_ge(ctx_loaded, (b + 2) * 16)
                    for lt in range(2 * i, min(2 * i + 2, LT)):
                        r = rows_of(lt)
                        for k in range(KC):
                            mm = pe.matmul(spare[0:r, (lt % 2) * D:(lt % 2 + 1) * D], ctx_sb[:, k, lt * P:lt * P + r],
                                           wv_sb[:, k, :], start=(k == 0), stop=(k == KC - 1))
                elif name == "o_turn":
                    pe.wait_ge(acc_taken, b * G + i + 1 if i < G - 1 else b * G)
                    for t in range(NT):
                        mm = pe.transpose(spare[:, t * P:(t + 1) * P], o_acc[:, t * P:(t + 1) * P], ident[:, :])
                elif name == "attn_turn":
                    for t in range(NT):
                        mm = pe.transpose(spare[:, t * P:(t + 1) * P], attn[:, t, i * P:(i + 1) * P], ident[:, :])
                elif name == "out_proj":
                    for t in (2 * i, 2 * i + 1):
                        for k in range(KC):
                            mm = pe.matmul(spare[:, (t % 2) * D:(t % 2 + 1) * D], attn_t[:, k, t * P:(t + 1) * P],
                                           wo_sb[:, k, :], start=(k == 0), stop=(k == KC - 1))
                elif name == "row_turn":
                    pe.wait_ge(rows_ready, 2 * b)
                    for t in range(NT):
                        mm = pe.transpose(spare[:, t * P:(t + 1) * P], routed_rows[:, 0, t, i * P:(i + 1) * P], ident[:, :])
                elif name == "logits":
                    for t in range(NT // 2, NT):
                        for k in range(KC):
                            mm = pe.matmul(spare[:, t * E:(t + 1) * E], row_t[:, k, t * P:(t + 1) * P],
                                           router_sb[:, k, :], start=(k == 0), stop=(k == KC - 1))
                else:
                    pe.wait_ge(route_step, b * ROUTE_STEPS)
                    pe.matmul(spare[:, 0:NT * E], tri[:, :], chosen[:, :, :], start=True, stop=False)
                    mm = pe.matmul(spare[:, 0:NT * E], ones[:, :], seen_at[:, :, :], start=False, stop=True)
                mm.then_inc(fill_ready, 1)

            def first_logits(it):
                pe.wait_ge(fill_taken, it.made("logits", 0) - 1)
                for t in range(NT // 2):
                    for k in range(KC):
                        pe.matmul(spare[:, t * E:(t + 1) * E], row_t[:, k, t * P:(t + 1) * P],
                                  router_sb[:, k, :], start=(k == 0), stop=(k == KC - 1))

            def unit_scores(b, s, p):
                u = 2 * s + p
                g, lt = s // LT, s % LT
                if lt == 0 and p == 0:
                    pe.wait_ge(stack_in[g], (b + 1) * LOADS)
                wait(pe, exp_done, b * UNITS + (u - SLOTS + 1 if u >= SLOTS else (-1, 0, -2)[u]))
                for j in (2 * p, 2 * p + 1):
                    r = rows_of(lt)
                    mm = pe.matmul(scores[0:r, 2 * (u % SLOTS) + j % 2, :], k_stack[:, g, j, lt * P:lt * P + r],
                                   q_stack[:, g, j, :], start=True, stop=True)
                mm.then_inc(scores_ready, 1)

            def weigh(b, s):
                lt = s % LT
                r = rows_of(lt)
                pe.wait_ge(vz_ready, b * STEPS + s + 1)
                if lt == 0:
                    wait(pe, acc_taken, b * G + s // LT)
                for j in range(GH):
                    mm = pe.matmul(acc[32 * j:32 * j + 32, :], vz[0:r, s % RING, j, :], probs[0:r, s % RING, j, :],
                                   start=(lt == 0), stop=(lt == LT - 1))
                mm.then_inc(pv_done, 1)

            def run(it):
                for s in range(STEPS):
                    if s == SLOTS // 2 and it.cur and isinstance(it.b, int) and it.b == 0:
                        pe.wait_ge(fill_taken, it.base)
                    if it.cur:
                        unit_scores(it.b, s, 0)
                    if it.fill(s):
                        fill(it, *it.fill(s))
                    if it.tail and s == LOGITS - 1:
                        first_logits(it)
                    if it.cur:
                        unit_scores(it.b, s, 1)
                    if s >= 2 and it.cur:
                        weigh(it.b, s - 2)
                    if s < 2 and it.tail:
                        weigh(it.b - 1, STEPS + s - 2)

            over_batches(pe, run)
            pe.wait_ge(acc_taken, B * G)
            pe.wait_ge(route_step, B * ROUTE_STEPS)
            pe.matmul(acc[:, 0:E], ones[:, :], seen[:, :], start=True, stop=True).then_inc(counted, 1)

        @block.scalar
        def _(act):
            act.wait_ge(dve_setup, DVE_SETUP)
            act.wait_ge(gates_in, 32)
            act.activation(tgx[:, :], gx[:, :], ACT.Tanh).then_inc(tanh_ready, 1)
            act.activation(tgf[:, :], gf[:, :], ACT.Tanh).then_inc(tanh_ready, 1)

            def take(it, name, i):
                b = it.b
                if name in ("q", "k"):
                    c, at, n = it.chunk(name, i)
                    act.wait_ge(fill_ready, it.made(name, i))
                    if not it.first:
                        wait(act, parts_stored[c % 2], ((b + 1) * (CHUNKS // 2) + c // 2) * 16)
                    act.activation(parts_of(it, c)[:, 0, 0:n], bank(it, name, i)[:, 0:n], ACT.Copy,
                                   scale=D ** -0.5 if name == "q" else 1.0).then_inc(high_ready, 1)
                elif name == "v":
                    act.wait_ge(fill_ready, it.made(name, i))
                    if i == 0 and (not isinstance(b, int) or b > 0):
                        act.wait_ge(vz_ready, b * STEPS)
                    m = min(2, LT - 2 * i)
                    r = rows_of(2 * i) if m == 1 else P
                    act.copy(v_ones[0:r, (b + 1) % 2, 2 * i:2 * i + m, :, 0:DH],
                             bank(it, name, i)[0:r, 0:m * D].rearrange("p (t h c) -> p t h c", t=m, h=H)).then_inc(fill_taken, 1)
                elif name == "x_turn":
                    act.wait_ge(fill_ready, it.made(name, i))
                    act.copy(x_t[:, i, :], spare[:, :]).then_inc(fill_taken, 1)
                elif name == "logits":
                    act.wait_ge(fill_taken, it.made("logits", 0))
                    act.activation(prob[:, 1, :, :], prob[:, 0, :, :], ACT.Exp).then_inc(route_exp, 1)

            def load_experts():
                act.wait_ge(scores_ready, B * UNITS)
                act.wait_ge(vz_ready, B * STEPS)
                act.wait_ge(pv_done, B * STEPS)
                for e in range(E):
                    if e >= EARLY_W1:
                        load_w1(act, e)
                    act.dma_start(w2_all[:, e * HC * D:(e + 1) * HC * D].rearrange("p (k c) -> p k c", k=HC),
                                  w2[e].rearrange("(k p) c -> p k c", p=P)).then_inc(expert_in[e], 16)

            def run(it):
                b = it.b
                if isinstance(b, int) and b == B:
                    load_experts()
                if isinstance(b, int) and b == 0:
                    for half in range(2):
                        act.wait_ge(parts_stored[half], CHUNKS // 2 * 16)
                for s in range(STEPS):
                    if s < STEPS - 1 and it.fill(s) and it.fill(s)[0] != "logits":
                        take(it, *it.fill(s))
                    if s == LOGITS + 1 and it.tail:
                        take(it, "logits", 0)
                    if not it.cur:
                        continue
                    for p in range(2):
                        u = 2 * s + p
                        lt = s % LT
                        r = rows_of(lt)
                        act.wait_ge(negmax_ready, b * UNITS + u + 1)
                        if p == 0:
                            wait(act, pv_done, b * STEPS + s - RING + 1)
                        for j in (2 * p, 2 * p + 1):
                            e = act.activation(probs[0:r, s % RING, j, :], scores[0:r, 2 * (u % SLOTS) + j % 2, :],
                                               ACT.Exp, bias=negmax[0:r, u % 4, j % 2:j % 2 + 1],
                                               accum_out=z[0:r, s % RING, j:j + 1])
                        e.then_inc(exp_done, 1)
                    if s == STEPS - 1 and it.fill(s):
                        take(it, *it.fill(s))

            over_batches(act, run)

        @block.vector
        def _(dve):
            for tile, value in ((v_ones[:, :, :, :, DH], 1.0), (vz[:, :, :, :], 0.0), (minus_half[:, :], -0.5),
                                (zero[:, :], 0.0), (seen[:, :], 0.0), (ones_e[:, :], 1.0)):
                dve.memset(tile, value).then_inc(dve_setup, 1)
            for e in range(E):
                dve.memset(region_at[:, e:e + 1], float(e * REGION)).then_inc(dve_setup, 1)
                dve.memset(first_of[:, e:e + 1], float(E - e)).then_inc(dve_setup, 1)
            dve.wait_ge(dve_setup, DVE_SETUP)
            dve.wait_ge(tanh_ready, 2)
            dve.wait_ge(constants, 1)

            def bc(ap):
                return ap.unsqueeze(2).to_broadcast([P, NT, E])

            def pick(chain, k, values, free):
                chain(dve.tensor_reduce(top[:, k, :], values, AX.X, ALU.max))
                yield
                chain(dve.tensor_tensor(tmp[:, 0, :, :], values, bc(top[:, k, :]), ALU.is_equal))
                yield
                chain(dve.tensor_tensor(tmp[:, 0, :, :], tmp[:, 0, :, :],
                                        first_of[:, :].unsqueeze(1).to_broadcast([P, NT, E]), ALU.mult))
                yield
                chain(dve.tensor_reduce(top[:, free, :], tmp[:, 0, :, :], AX.X, ALU.max))
                yield
                chain(dve.tensor_tensor(one_hot[:, k, :, :], tmp[:, 0, :, :], bc(top[:, free, :]), ALU.is_equal))
                yield

            def take(it, name, i):
                b = it.b
                dve.wait_ge(fill_ready, it.made(name, i))
                if name in ("attn_turn", "row_turn"):
                    to = {"attn_turn": attn_t, "row_turn": row_t}[name]
                    dve.tensor_copy(to[:, i, :], spare[:, :]).then_inc(fill_taken, 1)
                elif name in ("q", "k"):
                    c, at, n = it.chunk(name, i)
                    dve.wait_ge(high_ready, (b + 1) * CHUNKS + at + 1)
                    if it.first and at >= 2:
                        dve.wait_ge(parts_ready, at - 1)
                    dve.scalar_tensor_tensor(out=resid[:, at % 2, 0:n], in0=bank(it, name, i)[:, 0:n],
                                             scalar=D ** -0.5 if name == "q" else 1.0, in1=parts_of(it, c)[:, 0, 0:n],
                                             op0=ALU.mult, op1=ALU.subtract).then_inc(fill_taken, 1)
                elif name == "o_turn":
                    of = spare[:, :].rearrange("p (t j c) -> p t j c", t=NT, j=GH)
                    dve.reciprocal(rden[:, :, :], of[:, :, :, DH]).then_inc(rden_ready, 1)
                    dve.wait_ge(rden_ready, b * G + i + 1 if i < G - 1 else b * G)
                    dve.tensor_tensor(attn[:, :, i * GH * DH:(i + 1) * GH * DH].rearrange("p t (j c) -> p t j c", j=GH),
                                      of[:, :, :, 0:DH], rden[:, :, :].unsqueeze(3).to_broadcast([P, NT, GH, DH]),
                                      ALU.mult).then_inc(fill_taken, 1)
                elif name == "out_proj":
                    if i == 0:
                        dve.wait_ge(x2_loaded, b * 16)
                    view = x2[:, 2 * i:2 * i + 2, :].rearrange("p t c -> p (t c)")
                    dve.scalar_tensor_tensor(out=view, in0=spare[:, :], scalar=tgx[:, 0:1], in1=view,
                                             op0=ALU.mult, op1=ALU.add).then_inc(fill_taken, 1)
                elif name == "logits":
                    lg = spare[:, 0:NT * E].rearrange("p (t e) -> p t e", t=NT)
                    dve.tensor_reduce(top[:, 7, :], lg, AX.X, ALU.max).then_inc(logits_max, 1)
                    dve.wait_ge(logits_max, b)
                    dve.tensor_tensor(prob[:, 0, :, :], lg, bc(top[:, 7, :]), ALU.subtract).then_inc(fill_taken, 1)
                elif name == "prefix":
                    dve.tensor_tensor(slot[:, :, :], spare[:, 0:NT * E].rearrange("p (t e) -> p t e", t=NT),
                                      region_at[:, :].unsqueeze(1).to_broadcast([P, NT, E]), ALU.add).then_inc(fill_taken, 1)

            def route(b, chain):
                dve.wait_ge(route_exp, b)
                chain(dve.tensor_reduce(top[:, 6, :], prob[:, 1, :, :], AX.X, ALU.add))
                yield
                chain(dve.reciprocal(top[:, 7, :], top[:, 6, :]))
                yield
                chain(dve.tensor_tensor(prob[:, 0, :, :], prob[:, 1, :, :], bc(top[:, 7, :]), ALU.mult))
                yield
                yield from pick(chain, 0, prob[:, 0, :, :], 2)
                chain(dve.tensor_scalar(tmp[:, 0, :, :], one_hot[:, 0, :, :], -2.0, None, ALU.mult))
                yield
                chain(dve.tensor_tensor(prob[:, 2, :, :], prob[:, 0, :, :], tmp[:, 0, :, :], ALU.add))
                yield
                yield from pick(chain, 1, prob[:, 2, :, :], 3)
                chain(dve.tensor_tensor(top[:, 6, :], top[:, 0, :], top[:, 1, :], ALU.add))
                yield
                chain(dve.reciprocal(top[:, 7, :], top[:, 6, :]))
                yield
                chain(dve.tensor_scalar(top[:, 7, :], top[:, 7, :], tgf[:, 0:1], None, ALU.mult))
                yield
                chain(dve.tensor_tensor(top[:, 4:6, :], top[:, 0:2, :],
                                        top[:, 7, :].unsqueeze(1).to_broadcast([P, 2, NT]), ALU.mult))
                yield
                chain(dve.tensor_tensor(chosen[:, :, :], one_hot[:, 0, :, :], one_hot[:, 1, :, :], ALU.add))
                yield
                chain(dve.tensor_copy(seen_at[:, 0, :], seen[:, :]))
                yield
                for t in range(1, NT):
                    chain(dve.tensor_tensor(seen_at[:, t, :], seen_at[:, t - 1, :], chosen[:, t - 1, :], ALU.add))
                    yield
                chain(dve.tensor_tensor(seen[:, :], seen_at[:, NT - 1, :], chosen[:, NT - 1, :], ALU.add))
                yield

            def place_rows(it, chain):
                dve.wait_ge(fill_taken, it.made("prefix", 0))
                chain(dve.tensor_tensor(tmp[:, :, :, :], slot[:, :, :].unsqueeze(1).to_broadcast([P, 2, NT, E]),
                                        one_hot[:, :, :, :], ALU.mult))
                yield
                chain(dve.tensor_reduce(top[:, 6:8, :], tmp[:, :, :, :], AX.X, ALU.add))
                yield
                chain(dve.tensor_copy(place[:, :, :], top[:, 6:8, :]))
                yield
                chain(dve.tensor_copy(routed_rows[:, :, :, D], top[:, 4:6, :]))
                yield
                chain(dve.tensor_copy(routed_rows[:, :, :, D + 1].bitcast(U32),
                                      token[:, :].unsqueeze(1).to_broadcast([P, 2, NT])))
                yield
                chain(dve.tensor_scalar(token[:, :], token[:, :], float(N), None, ALU.add))
                yield

            def reciprocals(b, s):
                r = rows_of(s % LT)
                dve.wait_ge(exp_done, b * UNITS + 2 * s + 2)
                dve.reciprocal(rz[0:r, s % RING, :], z[0:r, s % RING, :]).then_inc(rz_ready, 1)

            def take_acc(b, g):
                dve.wait_ge(pv_done, b * STEPS + (g + 1) * LT)
                dve.tensor_copy(o_acc[:, :], acc[:, :]).then_inc(acc_taken, 1)

            def run(it):
                b = it.b
                for s in range(STEPS):
                    for p in range(2):
                        if it.cur:
                            u = 2 * s + p
                            r = rows_of(s % LT)
                            dve.wait_ge(scores_ready, b * UNITS + u + 1)
                            dve.tensor_reduce(negmax[0:r, u % 4, :], scores[0:r, 2 * (u % SLOTS):2 * (u % SLOTS) + 2, :],
                                              AX.X, ALU.max, negate=True).then_inc(negmax_ready, 1)
                        if p == 1 and s == 1 and it.tail:
                            take_acc(b - 1, G - 1)
                        if p == 1 and it.cur and s in (LT + 1, 2 * LT + 1, 3 * LT + 1):
                            take_acc(b, s // LT - 1)
                        if p == 1 and s == 0 and it.tail:
                            reciprocals(b - 1, STEPS - 1)
                        if p == 1 and s > 0 and it.cur:
                            reciprocals(b, s - 1)
                        f = it.fill(s)
                        if f and f[0] not in ("v", "x_turn") and p == (f[0] in ("q", "k")):
                            take(it, *f)
                        if p == 1 and it.tail and s == OUT:
                            dve.wait_ge(fill_taken, it.made("out_proj", 1))
                        if p == 1 and it.tail and s in (OUT + 1, OUT + 2):
                            for t in range(2 * (s - OUT - 1), 2 * (s - OUT)):
                                dve.bn_stats(stats2[:, t, :], x2[:, t, :]).then_inc(stats2_done, 1)
                        if p == 1 and it.tail and s == OUT + 3:
                            wait_apart(dve, stats2_done, b * NT, passed_dve)
                            for t in range(NT):
                                dve.bn_aggr(mv2[:, t, :], stats2[:, t, :]).then_inc(mv2_ready, 1)
                        if p == 0 and it.next and s in STATS_X:
                            t = STATS_X.index(s)
                            if t == 0:
                                dve.wait_ge(x_loaded, (b + 2) * 16)
                            dve.bn_stats(stats1[:, t, :], x_in[:, t, :]).then_inc(stats_done, 1)
                        if p == 1 and it.next and s == CENTRE_X - 1:
                            wait_apart(dve, stats_done, (b + 2) * NT, passed_dve)
                            for t in range(NT):
                                dve.bn_aggr(mv1[:, t, :], stats1[:, t, :]).then_inc(mv_ready, 1)
                        if it.tail and s == ROUTE and p == 0:
                            routing = Chain(dve, route_step, (b - 1) * ROUTE_STEPS)
                            route_steps = route(b, routing)
                        if it.tail and ROUTE <= s < ROUTE + (ROUTE_STEPS + 1) // 2:
                            in_turn(routing, route_steps)
                        if it.tail and s == PLACE and p == 0:
                            routing.settle()
                            placing = Chain(dve, place_step, (b - 1) * PLACE_STEPS)
                            place_steps = place_rows(it, placing)
                        if it.tail and PLACE <= s < PLACE + PLACE_STEPS // 2:
                            in_turn(placing, place_steps)

            over_batches(dve, run)

            steps = Chain(dve, plan_step, 0)

            def chain(ins):
                steps(ins)
                steps.settle()

            dve.wait_ge(counted, 1)
            chain(dve.tensor_copy(count[:, :], acc[:, 0:E]))
            chain(dve.tensor_tensor(pad_at[:, :], count[:, :], region_at[:, :], ALU.add))
            dve.tensor_copy(plan[:, 2 * NBLK:2 * NBLK + E], pad_at[:, :]).then_inc(pads_known, 1)
            chain(dve.tensor_scalar(count_up[:, :], count[:, :], float(BLK - 1), None, ALU.add))
            chain(dve.tensor_scalar(blocks_i[:, :], count_up[:, :], BLK.bit_length() - 1, None, ALU.logical_shift_right))
            chain(dve.tensor_copy(blocks_of[:, :], blocks_i[:, :]))
            chain(dve.tensor_tensor_scan(last_of[:, :], ones_e[:, :], blocks_of[:, :], 0.0, ALU.mult, ALU.add))
            chain(dve.tensor_tensor(past[:, :, :], number[:, :].unsqueeze(2).to_broadcast([P, NBLK, E]),
                                    last_of[:, :].unsqueeze(1).to_broadcast([P, NBLK, E]), ALU.is_ge))
            chain(dve.tensor_reduce(expert_f[:, :], past[:, :, :], AX.X, ALU.add))
            chain(dve.tensor_tensor(past[:, :, :], past[:, :, :],
                                    blocks_of[:, :].unsqueeze(1).to_broadcast([P, NBLK, E]), ALU.mult))
            chain(dve.tensor_reduce(first_f[:, :], past[:, :, :], AX.X, ALU.add))
            chain(dve.tensor_tensor(row_f[:, :], number[:, :], first_f[:, :], ALU.subtract))
            chain(dve.tensor_scalar(row_f[:, :], row_f[:, :], float(BLK), None, ALU.mult))
            chain(dve.tensor_scalar(first_f[:, :], expert_f[:, :], float(REGION), None, ALU.mult))
            chain(dve.tensor_tensor(row_f[:, :], row_f[:, :], first_f[:, :], ALU.add))
            chain(dve.tensor_scalar(row_f[:, :], row_f[:, :], float(SPARE), None, ALU.min))
            chain(dve.tensor_scalar(expert_f[:, :], expert_f[:, :], float(E - 1), None, ALU.min))
            chain(dve.tensor_copy(plan[:, 0:NBLK], expert_f[:, :]))
            chain(dve.tensor_copy(plan[:, NBLK:2 * NBLK], row_f[:, :]))

        @block.gpsimd
        def _(pool):
            pool.memset(ident[:, :], 0.0).then_inc(keep["built"], 1)
            pool.memset(tri[:, :], 1.0).then_inc(keep["built"], 1)
            pool.memset(ones[:, :], 1.0).then_inc(keep["built"], 1)
            pool.memset(pad_row[:, 0:D + 1], 0.0).then_inc(keep["built"], 1)
            pool.iota(token[:, :], pattern=[[P, NT]], base=0, channel_multiplier=1,
                      allow_small_or_imprecise_dtypes=True).then_inc(keep["built"], 1)
            pool.iota(number[:, :], pattern=[[1, NBLK]], base=0, channel_multiplier=0,
                      allow_small_or_imprecise_dtypes=True).then_inc(keep["built"], 1)
            pool.iota(pad_row[:, D + 1:D + 2].bitcast(U32), pattern=[[0, 1]], base=TOKENS,
                      channel_multiplier=1).then_inc(keep["built"], 1)
            pool.wait_ge(keep["built"], 7)
            pool.affine_select(out=ident[:, :], in_=ident[:, :], compare_op=ALU.not_equal, fill=1.0, base=0,
                               pattern=[[-1, P]], channel_multiplier=1).then_inc(keep["built"], 1)
            pool.affine_select(out=tri[:, :], in_=tri[:, :], compare_op=ALU.is_gt, fill=0.0, base=0,
                               pattern=[[1, P]], channel_multiplier=-1).then_inc(keep["built"], 1)
            pool.wait_ge(keep["built"], 9)
            pool.drain().then_inc(constants, 1)
            pool.dma_start(out[TOKENS:TOKENS + P, :], pad_row[:, 0:D]).then_inc(rows_out, 16)
            pool.wait_ge(dve_setup, DVE_SETUP)

            def one_over_deviation(mv, rstd, step, before):
                pool.tensor_scalar(rstd[:, 0, :], mv[:, :, 1], EPS, None, ALU.add).then_inc(step, 1)
                pool.wait_ge(step, before + 1)
                pool.tensor_tensor(rstd[:, 1, :], rstd[:, 0, :], minus_half[:, :], ALU.pow).then_inc(step, 1)
                pool.wait_ge(step, before + 2)

            def by_row(op, out, in0, factor, half):
                t = slice(2 * half, 2 * half + 2)
                return pool.tensor_tensor(out[:, t, 0:D], in0[:, t, 0:D], factor[:, t].unsqueeze(2).to_broadcast([P, 2, D]), op)

            def weigh_values(b, s):
                g, lt = s // LT, s % LT
                r = rows_of(lt)
                pool.wait_ge(rz_ready, b * STEPS + s + 1)
                wait(pool, pv_done, b * STEPS + s - RING + 1)
                pool.tensor_tensor(vz[0:r, s % RING, :, 0:DH + 1], v_ones[0:r, b % 2, lt, g * GH:(g + 1) * GH, :],
                                   rz[0:r, s % RING, :].unsqueeze(2).to_broadcast([r, GH, DH + 1]),
                                   ALU.mult).then_inc(vz_ready, 1)

            def run(it):
                b = it.b
                for s in range(STEPS):
                    if s == 0 and it.cur:
                        pool.wait_ge(fill_taken, it.base)
                    if it.cur and s >= 1:
                        weigh_values(b, s - 1)
                    if it.tail and s == 0:
                        weigh_values(b - 1, STEPS - 1)
                    if it.tail and s == OUT + 4:
                        wait_apart(pool, mv2_ready, b * NT, passed_pool)
                        one_over_deviation(mv2, rstd2, rstd2_step, (b - 1) * 2)
                        pool.wait_ge(rows_out, (b - 1) * 2 * NT * 16 + 16)
                    if it.tail and s in (OUT + 4, OUT + 5):
                        by_row(ALU.subtract, routed_rows[:, 1, :, :], x2, mv2[:, :, 0], s - OUT - 4).then_inc(centred2, 1)
                    if it.tail and s in (OUT + 5, OUT + 6):
                        pool.wait_ge(centred2, 2 * b)
                        by_row(ALU.mult, routed_rows[:, 0, :, :], routed_rows[:, 1, :, :], rstd2[:, 1, :], s - OUT - 5).then_inc(rows_ready, 1)
                    if it.tail and s in (OUT + 6, OUT + 7):
                        pool.wait_ge(rows_ready, 2 * b)
                        by_row(ALU.mult, routed_rows[:, 1, :, :], routed_rows[:, 1, :, :], rstd2[:, 1, :], s - OUT - 6).then_inc(rows1_ready, 1)
                    if it.next and s == CENTRE_X:
                        wait_apart(pool, mv_ready, (b + 2) * NT, passed_pool)
                        one_over_deviation(mv1, rstd1, rstd_step, (b + 1) * 2)
                    if it.next and s in (CENTRE_X, CENTRE_X + 1):
                        by_row(ALU.subtract, x_in, x_in, mv1[:, :, 0], s - CENTRE_X).then_inc(centred1, 1)
                    if it.next and s in (CENTRE_X + 2, CENTRE_X + 3):
                        pool.wait_ge(centred1, 2 * (b + 2))
                        by_row(ALU.mult, x_in, x_in, rstd1[:, 1, :], s - CENTRE_X - 2).then_inc(xn_ready, 1)
                    f = it.fill(s - 1) if s else None
                    if f and f[0] in ("q", "k"):
                        name, i = f
                        c, at, n = it.chunk(name, i)
                        pool.wait_ge(middle_ready, (b + 1) * CHUNKS + at + 1)
                        pool.tensor_tensor(parts_of(it, c)[:, 2, 0:n], resid[:, at % 2, 0:n], parts_of(it, c)[:, 1, 0:n],
                                           ALU.subtract).then_inc(parts_ready, 1)
                    f = it.fill(s)
                    if f and f[0] in ("q", "k"):
                        name, i = f
                        c, at, n = it.chunk(name, i)
                        pool.wait_ge(fill_taken, it.made(name, i))
                        pool.tensor_tensor(parts_of(it, c)[:, 1, 0:n], resid[:, at % 2, 0:n], zero[:, 0:1].to_broadcast([P, n]),
                                           ALU.add).then_inc(middle_ready, 1)
                    if it.tail and STEPS - 2 * NT <= s:
                        k, t = (s - STEPS + 2 * NT) // NT, (s - STEPS + 2 * NT) % NT
                        if s == STEPS - 2 * NT:
                            pool.wait_ge(rows1_ready, 2 * b)
                            wait_apart(pool, place_step, b * PLACE_STEPS, passed_pool)
                        pool.indirect_dma_start(
                            out=routed, out_offset=bass.IndirectOffsetOnAxis(place[:, k, t:t + 1], 0),
                            in_=routed_rows[:, k, t, :], in_offset=None).then_inc(rows_out, 16)

            over_batches(pool, run)
            pool.wait_ge(rows_out, B * 2 * NT * 16 + 16)


def experts(nc, keep, routed, out):
    ident, plan, w1_all, w2_all = (keep[name] for name in ("ident", "plan", "w1_all", "w2_all"))
    pads_in, expert_in = keep["pads_in"], keep["expert_in"]
    MIDDLE = NBLK - 5
    BANKS = HC * BLK // 512
    HB = HC // BANKS
    assert MIDDLE % 2 == 0 and BLK == P

    with ExitStack() as ctx:
        def sb(name, shape, dt=F32):
            return ctx.enter_context(nc.sbuf_tensor(name, shape, dt))

        def psum(name, shape):
            return ctx.enter_context(nc.psum_tensor(name, shape, F32))

        def sem(name):
            return ctx.enter_context(nc.semaphore(name))

        rows = sb("rows", [P, 2, ROW])
        w1_sb = sb("w1_sb", [P, 2, KC * HID])
        w2_sb = sb("w2_sb", [P, 2, HC * D])
        rows_t = sb("rows_t", [P, 2, KC * BLK])
        hidden = sb("hidden", [P, 2, HC * BLK])
        gate_token = sb("gate_token", [P, 2, 2])
        result = sb("result", [P, 2, D])

        ps_rows = psum("ps_rows", [P, 512])
        ps_hidden = psum("ps_hidden", [P, 2 * BANKS, 512])
        ps_y = psum("ps_y", [P, 2, 512])

        rows_in = [sem(f"rows_in_{slot}") for slot in range(2)]
        experts_here = sem("experts_here")
        w1_ready = sem("w1_ready")
        w2_ready = sem("w2_ready")
        turned = sem("turned")
        rows_taken = sem("rows_taken")
        gates_taken = sem("gates_taken")
        hidden_ready = sem("hidden_ready")
        gelu_done = sem("gelu_done")
        y_ready = sem("y_ready")
        scaled = sem("scaled")
        added = sem("added")
        passed_pool, passed_dve = (sem(f"passed_in_experts_{e}") for e in ("pool", "dve"))

        block = ctx.enter_context(nc.Block())

        def over_blocks(eng, run):
            run(1, 1, False)
            run(2, 0, False)
            with eng.Fori(0, MIDDLE // 2) as i:
                run(i * 2 + 3, 1, False)
                run(i * 2 + 4, 0, False)
            run(NBLK - 2, (NBLK - 2) % 2, False)
            run(NBLK - 1, (NBLK - 1) % 2, True)

        @block.sync
        def _(sp):
            sp.wait_ge(pads_in, (E + 1) * 16)

            def load(j, slot):
                at = nc.values_load(plan[0:1, bass.ds(j + NBLK, 1)], engines=[SP_ENGINE], min_val=0, max_val=SPARE)
                wait(sp, rows_taken, j - 1)
                wait(sp, gates_taken, j - 1)
                sp.dma_start(rows[:, slot, :], routed[bass.ds(at, BLK), :]).then_inc(rows_in[slot], 16)

            load(0, 0)
            load(1, 1)
            with sp.Fori(0, (NBLK - 3) // 2) as i:
                load(i * 2 + 2, 0)
                load(i * 2 + 3, 1)
            load(NBLK - 1, (NBLK - 1) % 2)

        @block.tensor
        def _(pe):
            def turn(j, slot):
                pe.wait_ge(rows_in[slot], (j // 2 + 1) * 16)
                wait(pe, rows_taken, j)
                for k in range(KC):
                    mm = pe.transpose(ps_rows[:, k * BLK:(k + 1) * BLK], rows[:, slot, k * P:(k + 1) * P], ident[:, :])
                mm.then_inc(turned, 1)

            def first(j, slot):
                pe.wait_ge(rows_taken, j + 1)
                pe.wait_ge(w1_ready, j + 1)
                wait(pe, gelu_done, (j - 1) * BANKS)
                for h in range(HC):
                    for k in range(KC):
                        mm = pe.matmul(ps_hidden[:, slot * BANKS + h // HB, (h % HB) * BLK:(h % HB + 1) * BLK],
                                       w1_sb[:, slot, k * HID + h * P:k * HID + (h + 1) * P],
                                       rows_t[:, slot, k * BLK:(k + 1) * BLK], start=(k == 0), stop=(k == KC - 1))
                    if h % HB == HB - 1:
                        mm.then_inc(hidden_ready, 1)

            def second(j, slot):
                pe.wait_ge(w2_ready, j + 1)
                wait(pe, scaled, j - 1)
                for h in range(HC):
                    if h % HB == 0:
                        pe.wait_ge(gelu_done, j * BANKS + h // HB + 1)
                    mm = pe.matmul(ps_y[:, slot, 0:D], hidden[:, slot, h * BLK:(h + 1) * BLK],
                                   w2_sb[:, slot, h * D:(h + 1) * D], start=(h == 0), stop=(h == HC - 1))
                mm.then_inc(y_ready, 1)

            def run(j, slot, last):
                first(j, slot)
                if not last:
                    turn(j + 1, 1 - slot)
                second(j - 1, 1 - slot)

            turn(0, 0)
            first(0, 0)
            turn(1, 1)
            over_blocks(pe, run)
            second(NBLK - 1, (NBLK - 1) % 2)

        @block.scalar
        def _(act):
            def run(j, slot, last):
                for q in range(BANKS):
                    act.wait_ge(hidden_ready, j * BANKS + q + 1)
                    if q == 0:
                        wait(act, y_ready, j - 1)
                    act.activation(hidden[:, slot, q * 512:(q + 1) * 512], ps_hidden[:, slot * BANKS + q, :],
                                   ACT.Gelu).then_inc(gelu_done, 1)

            run(0, 0, False)
            over_blocks(act, run)

        @block.vector
        def _(dve):
            def expert(j):
                e = nc.values_load(plan[0:1, bass.ds(j, 1)], engines=[DVE_ENGINE], min_val=0, max_val=E - 1)
                wait_apart(dve, experts_here, e + 1, passed_dve)
                return e

            def take_w1(j, slot, e):
                wait(dve, hidden_ready, (j - 1) * BANKS)
                dve.tensor_copy(w1_sb[:, slot, :], w1_all[:, bass.ds(e * (KC * HID), KC * HID)]).then_inc(w1_ready, 1)

            def take_w2(j, slot, e):
                wait(dve, y_ready, j - 1)
                dve.tensor_copy(w2_sb[:, slot, :], w2_all[:, bass.ds(e * (HC * D), HC * D)]).then_inc(w2_ready, 1)

            def take_rows(j, slot):
                dve.wait_ge(turned, j + 1)
                dve.tensor_copy(rows_t[:, slot, :], ps_rows[:, 0:KC * BLK]).then_inc(rows_taken, 1)

            def take_gates(j, slot):
                wait(dve, added, (j - 1) * 16)
                dve.wait_ge(rows_in[slot], (j // 2 + 1) * 16)
                dve.tensor_copy(gate_token[:, slot, :], rows[:, slot, D:ROW]).then_inc(gates_taken, 1)

            def scale(j, slot):
                dve.wait_ge(y_ready, j + 1)
                dve.wait_ge(gates_taken, j + 1)
                wait(dve, added, (j - 1) * 16)
                dve.tensor_scalar(result[:, slot, :], ps_y[:, slot, 0:D], gate_token[:, slot, 0:1], None,
                                  ALU.mult).then_inc(scaled, 1)

            def run(j, slot, last):
                if not last:
                    e = expert(j + 1)
                    take_w1(j + 1, 1 - slot, e)
                take_gates(j, slot)
                if not last:
                    take_rows(j + 1, 1 - slot)
                scale(j - 1, 1 - slot)
                if not last:
                    take_w2(j + 1, 1 - slot, e)

            e = expert(0)
            take_w1(0, 0, e)
            take_rows(0, 0)
            take_w2(0, 0, e)
            take_gates(0, 0)
            e = expert(1)
            take_w1(1, 1, e)
            take_rows(1, 1)
            take_w2(1, 1, e)
            over_blocks(dve, run)
            scale(NBLK - 1, (NBLK - 1) % 2)

        @block.gpsimd
        def _(pool):
            for e in range(E):
                pool.wait_ge(expert_in[e], 32)
                pool.sem_inc(experts_here, 1)

            def add(j, slot):
                pool.wait_ge(scaled, j + 1)
                if not isinstance(j, int) or j > 0:
                    wait_apart(pool, added, j * 16, passed_pool)
                pool.indirect_dma_start(
                    out=out, out_offset=bass.IndirectOffsetOnAxis(gate_token[:, slot, 1:2].bitcast(U32), 0),
                    in_=result[:, slot, :], in_offset=None, compute_op=ALU.add).then_inc(added, 16)

            add(0, 0)
            over_blocks(pool, lambda j, slot, last: add(j, slot))
            pool.wait_ge(added, NBLK * 16)


def flamingo_block(nc, x, ctx_t, g_xattn, g_ffn, wq_t, wk_t, wv_t, wo_t, router_t, w1, w2, out):
    routed = nc.dram_tensor("routed", (SPARE + BLK, ROW), F32, kind="Internal").ap()
    q_parts_dram = nc.dram_tensor("q_parts", (3, D, N), BF16, kind="Internal").ap()
    k_parts_dram = nc.dram_tensor("k_parts", (3, D, L), BF16, kind="Internal").ap()
    with ExitStack() as ctx:
        keep = {name: ctx.enter_context(nc.sbuf_tensor(name, [P, n], dt))
                for name, n, dt in (("ident", P, F32), ("tri", P, F32), ("ones", P, F32), ("pad_row", ROW, F32),
                                    ("plan", 3 * NBLK, I32), ("w1_all", E * KC * HID, F32),
                                    ("w2_all", E * HC * D, F32))}
        for name in ("built", "pads_in"):
            keep[name] = ctx.enter_context(nc.semaphore(name))
        keep["expert_in"] = [ctx.enter_context(nc.semaphore(f"expert_in_{e}")) for e in range(E)]
        attention_and_routing(nc, keep, x, ctx_t, g_xattn, g_ffn, wq_t, wk_t, wv_t, wo_t, router_t, w1, w2,
                              out, routed, q_parts_dram, k_parts_dram)
        experts(nc, keep, routed, out)


def kernel(**inputs):
    import numpy as np
    import concourse.bacc as bacc
    from concourse.bass_utils import run_bass_kernel_spmd

    def turned(a):
        return np.ascontiguousarray(np.swapaxes(np.asarray(a), -1, -2))

    nc = bacc.Bacc("TRN2", target_bir_lowering=False, num_devices=1)
    given = [
        ("x", np.ascontiguousarray(inputs["x"])),
        ("ctx_t", turned(inputs["ctx_1024"])),
        ("g_xattn", np.ascontiguousarray(inputs["g_xattn"])),
        ("g_ffn", np.ascontiguousarray(inputs["g_ffn"])),
        ("wq_t", turned(inputs["L0_xattn_Wq"])),
        ("wk_t", turned(inputs["L0_xattn_Wk"])),
        ("wv_t", turned(inputs["L0_xattn_Wv"])),
        ("wo_t", turned(inputs["L0_xattn_Wo"])),
        ("router_t", turned(inputs["L0_ffn_router_w"])),
        ("w1", np.ascontiguousarray(inputs["L0_ffn_w1"])),
        ("w2", np.ascontiguousarray(inputs["L0_ffn_w2"])),
    ]
    arrays = {f"in_{name}": a for name, a in given}
    args = [nc.dram_tensor(f"in_{name}", a.shape, mybir.dt.from_np(a.dtype), kind="ExternalInput").ap()
            for name, a in given]
    out = nc.dram_tensor("out", (TOKENS + P, D), F32, kind="ExternalOutput").ap()
    flamingo_block(nc, *args, out)
    r = run_bass_kernel_spmd(nc, [arrays], core_ids=[0])
    return r.results[0]["out"][0:TOKENS].reshape(B, N, D)
```
